# Optimizing a Trainium2 kernel written in Bass

```python
import numpy as np
import jax
import jax.numpy as jnp

def _softmax(x, axis=-1):
    return jax.nn.softmax(x, axis=axis)

def _gelu(x):
    return jax.nn.gelu(x, approximate=True)

def _silu(x):
    return jax.nn.silu(x)

def _sigmoid(x):
    return jax.nn.sigmoid(x)

def _layernorm(x, axis=-1, eps=1e-05):
    m = jnp.mean(x, axis=axis, keepdims=True)
    v = jnp.var(x, axis=axis, keepdims=True)
    return (x - m) / jnp.sqrt(v + eps)

def _scatter_add(tgt, idx, src, axis=0):
    return tgt.at[idx].add(src)

def _segment_sum(src, seg, n):
    return jax.ops.segment_sum(src, seg, n)
kernel_name = 'mk_flamingo_gated_d1_seqx_r4_1cbab5'

def setup_inputs(seed: int=0):
    np.random.seed(seed)
    _w = jnp.asarray

    def _rec_inputs():
        import jax
        import jax.numpy as jnp
        _rk = jax.random.key(seed)
        x = -0.0002928 + 1 * jax.random.normal(jax.random.fold_in(_rk, 1), (2, 1024, 256), jnp.float32)
        _lenS = 1024 - jax.random.randint(jax.random.fold_in(_rk, 7), (2,), 0, max(1, 1024 // 4) + 1, jnp.int32)
        _lenS2 = 64 - jax.random.randint(jax.random.fold_in(_rk, 8), (2,), 0, max(1, 64 // 4) + 1, jnp.int32)
        _ctx_1024P = jax.random.normal(jax.random.fold_in(_rk, 11), (2, 16, 256), jnp.float32)
        _ctx_1024c = jax.random.dirichlet(jax.random.fold_in(_rk, 511), 0.3 * jnp.ones((16,), jnp.float32), (2, 64))
        _ctx_1024t = jnp.einsum('bsk,bkd->bsd', _ctx_1024c, _ctx_1024P)
        _ctx_1024t = _ctx_1024t * jax.lax.rsqrt(jnp.mean(jnp.square(_ctx_1024t)) + 1e-12) * 0.953939
        ctx_1024 = -1.39393e-06 + 0.999914 * (_ctx_1024t + 0.3 * jax.random.normal(jax.random.fold_in(_rk, 611), (2, 64, 256), jnp.float32))
        _g = jax.random.normal(jax.random.fold_in(_rk, 9001), (2, 1), jnp.float32)
        _g = jnp.sign(_g) * jnp.maximum(jnp.abs(_g), 1.0) + (_g == 0) * 1.0
        g_xattn = _g[0]
        g_ffn = _g[1]
        return (x, ctx_1024, g_xattn, g_ffn)
    x, ctx_1024, g_xattn, g_ffn = _rec_inputs()

    def _L0_xattn_setup():
        import jax, jax.numpy as jnp
        import numpy as np
        B, N, D_MODEL, H, DH = (2, 512, 256, 16, 64)
        SCALE = DH ** (-0.5)
        key = jax.random.key(seed)
        ks = jax.random.split(key, 6)

        def lin(k, fan_in, shape):
            return jax.random.normal(k, shape, dtype=jnp.float32) / np.sqrt(fan_in)
        return {'x': jax.random.normal(ks[0], (B, N, D_MODEL), dtype=jnp.float32), 'context': jax.random.normal(ks[1], (B, N, D_MODEL), dtype=jnp.float32), 'Wq': lin(ks[2], D_MODEL, (D_MODEL, H * DH)), 'Wk': lin(ks[3], D_MODEL, (D_MODEL, H * DH)), 'Wv': lin(ks[4], D_MODEL, (D_MODEL, H * DH)), 'Wo': lin(ks[5], H * DH, (H * DH, D_MODEL)), 'bo': jnp.zeros((D_MODEL,), dtype=jnp.float32)}
    _L0_xattn_all = _L0_xattn_setup()
    _L0_xattn_in = {k: v for k, v in _L0_xattn_all.items() if k in ('Wq', 'Wk', 'Wv', 'Wo', 'bo')}
    del _L0_xattn_all

    def _L0_ffn_setup():
        import jax, jax.numpy as jnp
        import numpy as np
        B, T, H = (8, 512, 256)
        F = 1024
        E = 8
        TOP_K = 2
        key = jax.random.key(seed)
        ks = jax.random.split(key, 6)
        s_h = 1.0 / np.sqrt(H)
        s_f = 1.0 / np.sqrt(F)
        return {'hidden_states': jax.random.normal(ks[0], (B, T, H), dtype=jnp.float32), 'gate_w': jax.random.uniform(ks[1], (H, E), minval=-s_h, maxval=s_h, dtype=jnp.float32), 'w1': jax.random.uniform(ks[2], (E, H, F), minval=-s_h, maxval=s_h, dtype=jnp.float32), 'b1': jax.random.uniform(ks[3], (E, F), minval=-s_h, maxval=s_h, dtype=jnp.float32), 'w2': jax.random.uniform(ks[4], (E, F, H), minval=-s_f, maxval=s_f, dtype=jnp.float32), 'b2': jax.random.uniform(ks[5], (E, H), minval=-s_f, maxval=s_f, dtype=jnp.float32)}
    _L0_ffn_all = _L0_ffn_setup()
    _L0_ffn_in = {k: v for k, v in _L0_ffn_all.items() if k in ('gate_w', 'w1', 'b1', 'w2', 'b2')}
    del _L0_ffn_all
    return {'x': x, 'ctx_1024': ctx_1024, 'g_xattn': g_xattn, 'g_ffn': g_ffn, 'L0_xattn_Wq': _L0_xattn_in['Wq'], 'L0_xattn_Wk': _L0_xattn_in['Wk'], 'L0_xattn_Wv': _L0_xattn_in['Wv'], 'L0_xattn_Wo': _L0_xattn_in['Wo'], 'L0_xattn_bo': _L0_xattn_in['bo'], 'L0_ffn_gate_w': _L0_ffn_in['gate_w'], 'L0_ffn_w1': _L0_ffn_in['w1'], 'L0_ffn_b1': _L0_ffn_in['b1'], 'L0_ffn_w2': _L0_ffn_in['w2'], 'L0_ffn_b2': _L0_ffn_in['b2']}

def reference(x, ctx_1024, g_xattn, g_ffn, L0_xattn_Wq, L0_xattn_Wk, L0_xattn_Wv, L0_xattn_Wo, L0_xattn_bo, L0_ffn_gate_w, L0_ffn_w1, L0_ffn_b1, L0_ffn_w2, L0_ffn_b2):
    import jax
    import jax.numpy as jnp

    def _L0_xattn_ref(x, context, Wq, Wk, Wv, Wo, bo):
        import jax, jax.numpy as jnp
        import numpy as np
        B, N, D_MODEL, H, DH = (2, 512, 256, 16, 64)
        SCALE = DH ** (-0.5)
        b, n, _ = x.shape
        m = context.shape[1]
        q = (x @ Wq).reshape(b, n, H, DH)
        k = (context @ Wk * SCALE).reshape(b, m, H, DH)
        v = (context @ Wv).reshape(b, m, H, DH)
        scores = jnp.einsum('bihd,bjhd->bhij', q, k)
        attn = jax.nn.softmax(scores, axis=-1)
        out = jnp.einsum('bhij,bjhd->bihd', attn, v)
        out = out.reshape(b, n, H * DH)
        return out @ Wo + bo

    def _L0_ffn_ref(hidden_states, gate_w, w1, b1, w2, b2):
        import jax, jax.numpy as jnp
        import numpy as np
        B, T, H = (8, 512, 256)
        F = 1024
        E = 8
        TOP_K = 2
        b, t, h = hidden_states.shape
        seq_rep = hidden_states.mean(axis=1)
        router_logits = seq_rep @ gate_w
        probs = jax.nn.softmax(router_logits.astype(jnp.float32), axis=-1)
        top_w, top_i = jax.lax.top_k(probs, TOP_K)
        top_w = top_w / top_w.sum(axis=-1, keepdims=True)
        top_w = top_w.astype(hidden_states.dtype)
        combine = jnp.zeros((b, E), dtype=hidden_states.dtype)
        combine = combine.at[jnp.arange(b)[:, None], top_i].set(top_w)
        out = jnp.zeros_like(hidden_states)
        for e in range(E):
            hmid = jax.nn.gelu(jnp.einsum('bth,hf->btf', hidden_states, w1[e]) + b1[e], approximate=False)
            y = jnp.einsum('btf,fh->bth', hmid, w2[e]) + b2[e]
            out = out + combine[:, e][:, None, None] * y
        return out
    x = x + jnp.tanh(g_xattn[0]) * _L0_xattn_ref(_layernorm(x, axis=-1), ctx_1024, L0_xattn_Wq, L0_xattn_Wk, L0_xattn_Wv, L0_xattn_Wo, L0_xattn_bo)
    x = x + jnp.tanh(g_ffn[0]) * _L0_ffn_ref(_layernorm(x, axis=-1), L0_ffn_gate_w, L0_ffn_w1, L0_ffn_b1, L0_ffn_w2, L0_ffn_b2)
    return x

_drawn_inputs = setup_inputs


def setup_inputs(seed=0):
    import zlib

    import numpy as np

    out = dict(_drawn_inputs(seed))
    spreads = {'L0_xattn_bo': (0.0, 0.1)}
    factors = {'L0_ffn_b1': 7.112, 'L0_ffn_b2': 5.272}
    for name, (base, spread) in spreads.items():
        noise = np.random.default_rng([zlib.crc32(name.encode()), seed]).standard_normal(out[name].shape)
        drawn = base * np.exp(spread * noise) if base else spread * noise
        out[name] = jnp.asarray(drawn.astype(out[name].dtype))
    for name, factor in factors.items():
        out[name] = (out[name] * factor).astype(out[name].dtype)
    return out
```

```python
import concourse.bass as bass
from concourse import mybir
from contextlib import ExitStack


def gated_cross_attention_moe_kernel(nc, x, ctx_tokens, g_xattn, g_ffn, Wq, Wk, Wv, Wo, bo,
                                     gate_w, w1, b1, w2, b2, out):
    f32 = mybir.dt.float32
    f32r = mybir.dt.float32r
    u32 = mybir.dt.uint32
    ALU = mybir.AluOpType
    ACT = mybir.ActivationFunctionType
    AX = mybir.AxisListType.X
    ds = bass.ds

    P = 128
    B, S, D = x.shape
    M = ctx_tokens.shape[1]
    HD = Wq.shape[1]
    DH = 64
    H = HD // DH
    E, _, F = w1.shape
    TOP = 2
    NT = B * S // P
    TB = S // P
    KD = D // P
    NP = HD // P
    NF = F // P
    HM = H * M
    CH = 512
    NCH = S // CH
    BANK = 512
    NQ = B * TOP
    SCALE = DH ** -0.5
    EPS = 1e-5
    LEAD, LAG = 2, 3
    assert 2 * DH == P and 2 * M == P and B * M == P and TOP == 2 and NCH == 2 and KD == 2

    xf = x.rearrange("b s d -> (b s) d")

    cursor = [(nc.sbuf_base + 63) // 64 * 64]

    def place(name, shape, dtype=f32, at=None):
        size = 4
        for n in shape[1:]:
            size *= n
        offset = cursor[0] if at is None else at[0]
        t = nc.alloc_sbuf_tensor_at(name, shape, dtype, offset=offset)
        (cursor if at is None else at)[0] = offset + (size + 31) // 32 * 32
        return t

    xt = place("xt", [P, NT, D])
    yT_hi = place("yT_hi", [P, KD, NT * P], f32r)
    yT_lo = place("yT_lo", [P, KD, NT * P], f32r)
    ident = place("ident", [P, P])
    gate_sb = place("gate_sb", [P, KD, E])
    stats1 = place("stats1", [P, NT, 6])
    stats2 = stats1
    mean1 = place("mean1", [P, NT])
    rstd1 = place("rstd1", [P, NT])
    mean2 = place("mean2", [P, NT])
    rstd2 = place("rstd2", [P, NT])
    ve = place("ve", [P, NT])
    dm = place("dm", [P, NT])
    nu = place("nu", [P, NT])
    lnv = place("lnv", [P, NT])
    gg = place("gg", [P, 2])
    tg = place("tg", [P, 2])
    mx = place("mx", [P, 2, H])
    sm = place("sm", [P, 2, H])
    rs = place("rs", [P, 2, H])
    ysum = place("ysum", [P, KD, NT])
    rep = place("rep", [P, KD, B])
    row = place("row", [1, 16, B * E])
    idx = place("idx", [1, B * E], u32)
    hot = place("hot", [1, B * (TOP + 1), E])
    hotT = place("hotT", [E, B * (TOP + 1)])
    ones_row = place("ones_row", [1, P])
    iota_row = place("iota_row", [1, E])
    b1sel = place("b1sel", [P, NF, NQ])
    b2sel = place("b2sel", [P, KD, B])
    swt = place("swt", [P, NQ])
    bo_row = place("bo_row", [1, D])
    bo_parts = place("bo_parts", [1, 2 * D], f32r)
    one_r = place("one_r", [1, P], f32r)

    first = [cursor[0]]
    wq_sb = place("wq_sb", [P, KD, HD], at=first)
    wk_sb = place("wk_sb", [P, KD, HD], at=first)
    wv_sb = place("wv_sb", [P, KD, HD], at=first)
    wo_sb = place("wo_sb", [P, NP, D], at=first)
    wqT = place("wqT", [P, NP, D], at=first)
    kbd = place("kbd", [P, NP, B, P], at=first)
    vbd = place("vbd", [P, NP, B, P], at=first)
    ctx_sb = place("ctx_sb", [P, D], at=first)
    ctxT = place("ctxT", [P, KD, P], at=first)
    first2 = [cursor[0]]
    stage_w1 = [place("stage_w1_0", [P, KD, F], at=first2)]
    stage_w2 = [place("stage_w2_0", [P, NF, D], at=first2)]
    w1_hi = [place("w1_hi_0", [P, KD, F], f32r, at=first2)]
    w1_lo = [place("w1_lo_0", [P, KD, F], f32r, at=first2)]
    w2_hi = [place("w2_hi_0", [P, NF, D], f32r, at=first2)]
    w2_lo = [place("w2_lo_0", [P, NF, D], f32r, at=first2)]
    oT = place("oT", [P, KD, S], at=first2)

    second = [max(first[0], first2[0])]
    second2 = [second[0]]
    a_hi = place("a_hi", [P, KD, B * HM], f32r, at=second)
    a_lo = place("a_lo", [P, KD, B * HM], f32r, at=second)
    vw = place("vw", [P, B * NP, 2 * D], f32r, at=second)
    sx = place("sx", [P, 2, HM], at=second)
    third = [second[0]]
    pT_hi = place("pT_hi", [P, 2, NP, P], f32r, at=second)
    pT_lo = place("pT_lo", [P, 2, NP, P], f32r, at=second)
    xT_hi = place("xT_hi", [P, 2, KD, P], f32r, at=second)
    xT_lo = place("xT_lo", [P, 2, KD, P], f32r, at=second)
    xn = place("xn", [P, 2, D], at=second)
    stage_w1.append(place("stage_w1_1", [P, KD, F], at=second2))
    stage_w2.append(place("stage_w2_1", [P, NF, D], at=second2))
    w1_hi.append(place("w1_hi_1", [P, KD, F], f32r, at=second2))
    w1_lo.append(place("w1_lo_1", [P, KD, F], f32r, at=second2))
    w2_hi.append(place("w2_hi_1", [P, NF, D], f32r, at=second2))
    w2_lo.append(place("w2_lo_1", [P, NF, D], f32r, at=second2))
    gel = place("gel", [P, 2, CH], at=second2)
    h_hi = place("h_hi", [P, 4, CH], f32r, at=second2)
    h_lo = place("h_lo", [P, 4, CH], f32r, at=third)
    b1_sb = place("b1_sb", [E, F], at=third)
    b2_sb = place("b2_sb", [E, D], at=third)
    assert second2[0] <= third[0] and third[0] <= second[0]

    def as_f32(ap):
        return ap.bitcast(f32)

    stack = ExitStack()
    with stack:
        ps = stack.enter_context(nc.psum_tensor("ps", [P, 8, BANK], f32))

        def sem(name):
            return stack.enter_context(nc.semaphore(name))

        ld_ctx, ld_wk, ld_wq, ld_wv, ld_wo = (sem("ld_" + n) for n in ("ctx", "wk", "wq", "wv", "wo"))
        ld_x = [sem(f"ld_x_{b}") for b in range(B)]
        ld_small, ld_b12 = sem("ld_small"), sem("ld_b12")
        ident_ready, zeros_ready, rows_ready = sem("ident_ready"), sem("zeros_ready"), sem("rows_ready")
        tanh_done, tgbo_ready = sem("tanh_done"), sem("tgbo_ready")
        grp_done, grp_act, grp_dve = sem("grp_done"), sem("grp_act"), sem("grp_dve")
        grp_hi = sem("grp_hi")
        stats_done, ve_ready, ln_done, rs_done, ln_step = (
            sem(n) for n in ("stats_done", "ve_ready", "ln_done", "rs_done", "ln_step"))
        ln_ready, xc_ready = sem("ln_ready"), sem("xc_ready")
        xn_ready, xT_done, xhi_ready, xlo_ready = (
            sem(n) for n in ("xn_ready", "xT_done", "xhi_ready", "xlo_ready"))
        scores_done, head_done, max_done, sub_done, exp_done, sum_done, recip_done, mul_done = (
            sem(n) for n in ("scores_done", "head_done", "max_done", "sub_done", "exp_done", "sum_done",
                             "recip_done", "mul_done"))
        pT_done, phi_ready, plo_ready, out_done, x1a_done, x1_done = (
            sem(n) for n in ("pT_done", "phi_ready", "plo_ready", "out_done", "x1a_done", "x1_done"))
        y_ready, yT_done, yhi_ready, ylo_ready = (
            sem(n) for n in ("y_ready", "yT_done", "yhi_ready", "ylo_ready"))
        rep_ready, logits_done, route_step, route_exp, hot_ready, hotT_done, hotT_ready, sel_done, sel_ready = (
            sem(n) for n in ("rep_ready", "logits_done", "route_step", "route_exp", "hot_ready",
                             "hotT_done", "hotT_ready", "sel_done", "sel_ready"))
        staged = [sem("staged_0"), sem("staged_1")]
        w_hi_done, w_lo_done = sem("w_hi_done"), sem("w_lo_done")
        h_done, gelu_done, hhi_ready, hlo_ready, w2_done = (
            sem(n) for n in ("h_done", "gelu_done", "hhi_ready", "hlo_ready", "w2_done"))
        FREE_BANKS, FREE_GELS, FREE_SPLITS = 4, 2, 4
        FREE_SUM = 1
        oT_ready, oTT_done, x2_done, stored = (
            sem(n) for n in ("oT_ready", "oTT_done", "x2_done", "stored"))

        groups = ([("ctxT", 0)] + [("kT", i) for i in range(2)] + [("wqT", i) for i in range(4)]
                  + [("A", i) for i in range(8)] + [("vT", i) for i in range(2)]
                  + [("VW", i) for i in range(8)])
        number = {g: n for n, g in enumerate(groups)}
        EARLY = number[("vT", 0)]
        GRP_BANK = {g: n % 8 if n < EARLY else 4 + (n - EARLY) % 3 for n, g in enumerate(groups)}
        GRP_BEFORE = {g: next((h for h in reversed(groups[:n]) if GRP_BANK[h] == GRP_BANK[g]), None)
                      for n, g in enumerate(groups)}
        reader = {}
        counts = {"act": 0, "dve": 0}
        for kind, i in groups:
            who = "act" if kind in ("kT", "wqT", "vT") and i % 2 == 0 else "dve"
            counts[who] += 1
            reader[(kind, i)] = (who, counts[who])

        def wait_group_read(eng, kind, i):
            who, n = reader[(kind, i)]
            eng.wait_ge(grp_act if who == "act" else grp_dve, n)

        STEPS = list(range(-LEAD, NT + LAG))
        LOOP0, LOOP1 = LAG + 1, NT - LEAD

        def run_steps(eng, step, value_groups=lambda: None):
            for s in STEPS:
                if s == 1:
                    value_groups()
                if s < LOOP0:
                    step(s, s % 2)
            with eng.Fori(0, (LOOP1 - LOOP0) // 2) as i:
                step(LOOP0 + i * 2, 0)
                step(LOOP0 + 1 + i * 2, 1)
            for s in STEPS:
                if s >= LOOP1:
                    step(s, s % 2)

        def active(t):
            return not isinstance(t, int) or 0 <= t < NT

        def wait_pos(eng, s, v):
            if not isinstance(v, int) or v > 0:
                eng.wait_ge(s, v)

        block = stack.enter_context(nc.Block())

        @block.sync
        def _(sp):
            def load_x(b):
                sp.dma_start(xt[:, b * TB:(b + 1) * TB, :],
                             xf[b * S:(b + 1) * S, :].rearrange("(t p) d -> p t d", p=P)).then_inc(ld_x[b], 16)

            sp.dma_start(ctx_sb[:, :], ctx_tokens.rearrange("b m d -> (b m) d")).then_inc(ld_ctx, 16)
            sp.dma_start(wk_sb[:, :, :], Wk.rearrange("(k p) n -> p k n", p=P)).then_inc(ld_wk, 16)
            sp.dma_start(wq_sb[:, :, :], Wq.rearrange("(k p) n -> p k n", p=P)).then_inc(ld_wq, 16)
            load_x(0)
            sp.dma_start(wv_sb[:, :, :], Wv.rearrange("(k p) n -> p k n", p=P)).then_inc(ld_wv, 16)
            sp.dma_start(wo_sb[:, :, :], Wo.rearrange("(k p) n -> p k n", p=P)).then_inc(ld_wo, 16)
            load_x(1)

            sp.wait_ge(out_done, NT)
            sp.dma_start(b1_sb[:, :], b1).then_inc(ld_b12, 16)
            sp.dma_start(b2_sb[:, :], b2).then_inc(ld_b12, 16)

            sp.wait_ge(hot_ready, 1)
            for q in range(NQ):
                bq, slot = q // TOP, q % TOP
                e = sp.value_load(idx[0:1, bq * E + slot:bq * E + slot + 1], min_val=0, max_val=E - 1)
                if q >= TOP:
                    sp.wait_ge(w_lo_done, 2 + 2 * NCH * NF * (q - TOP))
                sp.dma_start(stage_w1[slot][:, :, :],
                             w1[ds(e, 1), :, :].rearrange("o (k p) n -> p (o k) n", p=P)).then_inc(staged[slot], 16)
                sp.dma_start(stage_w2[slot][:, :, :],
                             w2[ds(e, 1), :, :].rearrange("o (k p) n -> p (o k) n", p=P)).then_inc(staged[slot], 16)

            sp.wait_ge(w_lo_done, 2 + 2 * NCH * NF * TOP)
            sp.sem_inc(staged[0], 32)

            with sp.Fori(0, NT) as t:
                sp.wait_ge(x2_done, t + 1)
                sp.dma_start(out[ds(t * P, P), :],
                             xt[:, ds(t, 1), :].rearrange("p o d -> p (o d)")).then_inc(stored, 16)
            sp.wait_ge(stored, 16 * NT)

        @block.gpsimd
        def _(pool):
            nc.gpsimd.memset(ident[:, :], 0.0).then_inc(zeros_ready, 1)
            pool.wait_ge(zeros_ready, 1)
            nc.gpsimd.affine_select(out=ident[:, :], in_=ident[:, :], compare_op=ALU.not_equal, fill=1.0,
                                    base=0, pattern=[[-1, P]], channel_multiplier=1).then_inc(ident_ready, 1)
            nc.gpsimd.memset(kbd[:, :, :, :], 0.0).then_inc(zeros_ready, 1)
            nc.gpsimd.memset(vbd[:, :, :, :], 0.0).then_inc(zeros_ready, 1)
            nc.gpsimd.memset(ones_row[:, :], 1.0)
            for e in range(E):
                last = nc.gpsimd.memset(iota_row[:, e:e + 1], float(e))
            last.then_inc(rows_ready, 1)

            def step(s, par):
                t = s - 1
                if active(t):
                    q = (par - 1) % 2
                    pool.wait_ge(recip_done, t + 1)
                    pr = sx[:, q, :].rearrange("p (h m) -> p h m", m=M)
                    nc.gpsimd.tensor_tensor(pr, pr, rs[:, q, :].unsqueeze(2).broadcast_to([P, H, M]),
                                            ALU.mult).then_inc(mul_done, 1)
                t = s + LEAD
                if active(t):
                    wait_pos(pool, xT_done, t - 1)
                    tile = xt[:, ds(t, 1), :].rearrange("p o d -> p (o d)")
                    nc.gpsimd.tensor_tensor(xn[:, par, :], tile, mean1[:, ds(t, 1)].broadcast_to([P, D]),
                                            ALU.subtract).then_inc(xc_ready, 1)
                    pool.wait_ge(xc_ready, t + 1)
                    nc.gpsimd.tensor_tensor(xn[:, par, :], xn[:, par, :], rstd1[:, ds(t, 1)].broadcast_to([P, D]),
                                            ALU.mult).then_inc(xn_ready, 1)
            pool.wait_ge(ln_ready, 1)
            run_steps(pool, step)

        @block.scalar
        def _(act):
            act.dma_start(gg[:, 0:1], g_xattn.rearrange("(o n) -> o n", o=1).broadcast_to([P, 1])).then_inc(ld_small, 16)
            act.dma_start(gg[:, 1:2], g_ffn.rearrange("(o n) -> o n", o=1).broadcast_to([P, 1])).then_inc(ld_small, 16)
            act.dma_start(bo_row[:, :], bo.rearrange("(o n) -> o n", o=1)).then_inc(ld_small, 16)
            act.dma_start(gate_sb[:, :, :], gate_w.rearrange("(k p) e -> p k e", p=P)).then_inc(ld_small, 16)

            def rsqrt_guess(n):
                act.wait_ge(ve_ready, n)
                nc.scalar.activation(lnv[:, :], ve[:, :], ACT.Ln).then_inc(ln_done, 1)
                act.wait_ge(ln_done, n)
                nc.scalar.activation((rstd1 if n == 1 else rstd2)[:, :], lnv[:, :], ACT.Exp,
                                     scale=-0.5).then_inc(rs_done, 1)

            def group(kind, i):
                n = number[(kind, i)]
                bank = ps[:, GRP_BANK[(kind, i)], :]
                if kind in ("kT", "vT") and i % 2 == 0:
                    act.wait_ge(grp_done, n + 1)
                    act.wait_ge(zeros_ready, 3)
                    dst = kbd if kind == "kT" else vbd
                    for h in range(2):
                        r = slice(h * DH, (h + 1) * DH)
                        last = nc.scalar.activation(
                            dst[r, 4 * i:4 * i + 4, :, h * M:(h + 1) * M],
                            bank[r, :].rearrange("p (m b j) -> p m b j", m=4, b=B), ACT.Copy,
                            scale=SCALE if kind == "kT" else 1.0)
                    last.then_inc(grp_act, 1)
                if kind == "wqT" and i % 2 == 0:
                    act.wait_ge(grp_done, n + 1)
                    nc.scalar.activation(wqT[:, 2 * i:2 * i + 2, :],
                                         bank.rearrange("p (m c) -> p m c", m=2), ACT.Copy).then_inc(grp_act, 1)
                if kind == "A":
                    act.wait_ge(grp_done, n + 1)
                    ct, mp = i // 4, i % 4
                    dst = a_hi[:, ct, :].rearrange("p (b m x) -> p m b x", b=B, x=P)[:, 2 * mp:2 * mp + 2, :, :]
                    nc.scalar.activation(dst, bank.rearrange("p (m b x) -> p m b x", m=2, b=B),
                                         ACT.Copy).then_inc(grp_hi, 1)
                if kind == "VW":
                    act.wait_ge(grp_done, n + 1)
                    nc.scalar.activation(vw[:, 2 * i:2 * i + 2, 0:D], bank.rearrange("p (m n) -> p m n", m=2),
                                         ACT.Copy, scale=tg[:, 0:1]).then_inc(grp_hi, 1)

            for g in groups[:EARLY]:
                group(*g)
            act.wait_ge(ld_small, 64)
            nc.scalar.activation(tg[:, :], gg[:, :], ACT.Tanh).then_inc(tanh_done, 1)
            rsqrt_guess(1)

            def value_groups():
                act.wait_ge(tanh_done, 1)
                for g in groups[EARLY:]:
                    group(*g)

            def step(s, par):
                t = s - 2
                if active(t):
                    for half in range(2):
                        act.wait_ge(pT_done, 2 * t + half + 1)
                        if half == 0:
                            wait_pos(act, out_done, t - 1)
                        nc.scalar.activation(pT_hi[:, par, 4 * half:4 * half + 4, :],
                                             ps[:, 4 + half, :].rearrange("p (m i) -> p m i", m=4),
                                             ACT.Copy).then_inc(phi_ready, 1)
                t = s - 1
                if active(t):
                    q = (par - 1) % 2
                    act.wait_ge(sub_done, t + 1)
                    nc.scalar.activation(sx[:, q, 0:BANK], sx[:, q, 0:BANK], ACT.Exp).then_inc(exp_done, 1)
                t = s + 1
                if active(t):
                    q = (par + 1) % 2
                    act.wait_ge(xT_done, t + 1)
                    wait_pos(act, scores_done, t - 1)
                    nc.scalar.activation(xT_hi[:, q, :, :], ps[:, 7, 0:D].rearrange("p (k i) -> p k i", k=KD),
                                         ACT.Copy).then_inc(xhi_ready, 1)
                t = s
                if active(t):
                    act.wait_ge(max_done, t + 1)
                    wait_pos(act, pT_done, 2 * (t - 1))
                    for h in range(H // 2, H):
                        c0 = h * M
                        last = nc.scalar.activation(sx[:, par, c0:c0 + M], ps[:, 2 * par + 1, c0 - BANK:c0 - BANK + M],
                                                    ACT.Exp, bias=mx[:, par, h:h + 1],
                                                    accum_out=sm[:, par, h:h + 1])
                    last.then_inc(head_done, 1)
            run_steps(act, step, value_groups)

            rsqrt_guess(2)
            with act.Fori(0, NT // 2) as i:
                for par in range(2):
                    t = i * 2 + par
                    act.wait_ge(yT_done, t + 1)
                    for k in range(KD):
                        last = nc.scalar.activation(yT_hi[:, k, ds(t * P, P)], ps[:, 6 + par, k * P:(k + 1) * P],
                                                    ACT.Copy, accum_out=ysum[:, k, ds(t, 1)])
                    last.then_inc(yhi_ready, 1)

            act.wait_ge(route_step, 2)
            nc.scalar.activation(row[:, 2, :], row[:, 1, :], ACT.Exp).then_inc(route_exp, 1)

            act.wait_ge(staged[0], 32)
            act.wait_ge(sel_ready, 1)
            nc.scalar.activation(w1_hi[0][:, :, :], stage_w1[0][:, :, :], ACT.Copy).then_inc(w_hi_done, 1)
            nc.scalar.activation(w2_hi[0][:, :, :], stage_w2[0][:, :, :], ACT.Copy,
                                 scale=swt[:, 0:1]).then_inc(w_hi_done, 1)

            act.sem_inc(gelu_done, FREE_BANKS)
            with act.Fori(0, B) as b:
                for slot in range(TOP):
                    with act.Fori(0, NCH) as c:
                        for f in range(NF):
                            n = ((b * TOP + slot) * NCH + c) * NF + f
                            act.wait_ge(h_done, n + 1)
                            act.wait_ge(hlo_ready, n + 1)
                            nc.scalar.activation(gel[:, f % 2, :], ps[:, 4 + f % 4, :], ACT.Gelu,
                                                 bias=b1sel[:, f, ds(b * TOP + slot, 1)]).then_inc(gelu_done, 1)
                            nxt = 1 - slot
                            if f == 0:
                                act.wait_ge(w2_done, (b * TOP + slot) * NCH * NF + FREE_SPLITS)
                                act.wait_ge(staged[nxt], (b + 1 + slot) * 32)
                            nc.scalar.activation(w1_hi[nxt][:, ds(c, 1), f * P:(f + 1) * P],
                                                 stage_w1[nxt][:, ds(c, 1), f * P:(f + 1) * P],
                                                 ACT.Copy).then_inc(w_hi_done, 1)
                            sc = (b * TOP + slot + 1) if slot == 0 else b * 0 + (NQ // 2)
                            nc.scalar.activation(w2_hi[nxt][:, f, ds(c * P, P)],
                                                 stage_w2[nxt][:, f, ds(c * P, P)],
                                                 ACT.Copy, scale=swt[:, ds(sc, 1)]).then_inc(w_hi_done, 1)
                act.wait_ge(w2_done, (b + 1) * TOP * NCH * NF + FREE_SPLITS)
                act.wait_ge(oTT_done, b * TB + FREE_SUM)
                for c in range(NCH):
                    for d in range(KD):
                        nc.scalar.activation(oT[:, d, c * CH:(c + 1) * CH], ps[:, 2 * c + d, :], ACT.Identity,
                                             bias=b2sel[:, d, ds(b, 1)]).then_inc(oT_ready, 1)

        @block.vector
        def _(dve):
            def rstd_from(stats, mean, rstd, n):
                base = 7 * (n - 1)
                me, ce, mo, co = stats[:, :, 1], stats[:, :, 2], stats[:, :, 4], stats[:, :, 5]
                nc.vector.tensor_tensor(dm[:, :], me, mo, ALU.subtract).then_inc(ln_step, 1)
                nc.vector.tensor_tensor(mean[:, :], me, mo, ALU.add).then_inc(ln_step, 1)
                nc.vector.tensor_tensor(ve[:, :], ce, co, ALU.add).then_inc(ln_step, 1)
                dve.wait_ge(ln_step, base + 3)
                nc.vector.tensor_scalar(mean[:, :], mean[:, :], 0.5, None, ALU.mult)
                nc.vector.tensor_tensor(dm[:, :], dm[:, :], dm[:, :], ALU.mult)
                nc.vector.tensor_scalar(ve[:, :], ve[:, :], 1.0 / D, EPS, ALU.mult, ALU.add).then_inc(ln_step, 1)
                dve.wait_ge(ln_step, base + 4)
                nc.vector.scalar_tensor_tensor(ve[:, :], dm[:, :], 0.25, ve[:, :], ALU.mult, ALU.add).then_inc(ve_ready, 1)
                dve.wait_ge(ve_ready, n)
                dve.wait_ge(rs_done, n)
                nc.vector.scalar_tensor_tensor(nu[:, :], ve[:, :], -0.5, rstd[:, :], ALU.mult, ALU.mult).then_inc(ln_step, 1)
                dve.wait_ge(ln_step, base + 5)
                nc.vector.tensor_tensor(nu[:, :], nu[:, :], rstd[:, :], ALU.mult).then_inc(ln_step, 1)
                dve.wait_ge(ln_step, base + 6)
                nc.vector.scalar_tensor_tensor(rstd[:, :], nu[:, :], 1.5, rstd[:, :], ALU.add, ALU.mult).then_inc(ln_step, 1)
                dve.wait_ge(ln_step, base + 7)
                if n == 1:
                    dve.sem_inc(ln_ready, 1)

            def x_stats(b):
                dve.wait_ge(ld_x[b], 16)
                with dve.Fori(b * TB, (b + 1) * TB) as t:
                    nc.vector.bn_stats(stats1[:, ds(t, 1), :].rearrange("p o s -> p (o s)"),
                                       xt[:, ds(t, 1), :].rearrange("p o d -> p (o d)")).then_inc(stats_done, 1)

            def group(kind, i):
                n = number[(kind, i)]
                bank = ps[:, GRP_BANK[(kind, i)], :]
                if kind == "ctxT":
                    dve.wait_ge(grp_done, n + 1)
                    nc.vector.tensor_copy(ctxT[:, :, :], bank[:, 0:D].rearrange("p (k i) -> p k i", k=KD)).then_inc(grp_dve, 1)
                if kind in ("kT", "vT") and i % 2 == 1:
                    dve.wait_ge(grp_done, n + 1)
                    dve.wait_ge(zeros_ready, 3)
                    dst = kbd if kind == "kT" else vbd
                    for h in range(2):
                        r = slice(h * DH, (h + 1) * DH)
                        last = nc.vector.tensor_scalar(
                            dst[r, 4 * i:4 * i + 4, :, h * M:(h + 1) * M],
                            bank[r, :].rearrange("p (m b j) -> p m b j", m=4, b=B),
                            SCALE if kind == "kT" else 1.0, None, ALU.mult)
                    last.then_inc(grp_dve, 1)
                if kind == "wqT" and i % 2 == 1:
                    dve.wait_ge(grp_done, n + 1)
                    nc.vector.tensor_copy(wqT[:, 2 * i:2 * i + 2, :],
                                          bank.rearrange("p (m c) -> p m c", m=2)).then_inc(grp_dve, 1)
                if kind == "wqT" and i == 3:
                    for b in range(B):
                        x_stats(b)
                    dve.wait_ge(stats_done, NT)
                    rstd_from(stats1, mean1, rstd1, 1)
                if kind == "A":
                    ct, mp = i // 4, i % 4
                    view = [w[:, ct, :].rearrange("p (b m x) -> p m b x", b=B, x=P)[:, 2 * mp:2 * mp + 2, :, :]
                            for w in (a_hi, a_lo)]
                    dve.wait_ge(grp_hi, i + 1)
                    nc.vector.tensor_tensor(view[1], bank.rearrange("p (m b x) -> p m b x", m=2, b=B),
                                            as_f32(view[0]), ALU.subtract).then_inc(grp_dve, 1)
                if kind == "VW":
                    dve.wait_ge(grp_hi, 8 + i + 1)
                    nc.vector.scalar_tensor_tensor(vw[:, 2 * i:2 * i + 2, D:2 * D],
                                                   bank.rearrange("p (m n) -> p m n", m=2), tg[:, 0:1],
                                                   as_f32(vw[:, 2 * i:2 * i + 2, 0:D]), ALU.mult,
                                                   ALU.subtract).then_inc(grp_dve, 1)
            for g in groups[:EARLY]:
                group(*g)

            def value_groups():
                dve.wait_ge(tanh_done, 1)
                nc.vector.tensor_scalar(bo_parts[:, 0:D], bo_row[:, :], tg[0:1, 0:1], None, ALU.mult).then_inc(tgbo_ready, 1)
                dve.wait_ge(tgbo_ready, 1)
                nc.vector.scalar_tensor_tensor(bo_parts[:, D:2 * D], bo_row[:, :], tg[0:1, 0:1],
                                               as_f32(bo_parts[:, 0:D]), ALU.mult, ALU.subtract).then_inc(tgbo_ready, 1)
                dve.wait_ge(rows_ready, 1)
                nc.vector.tensor_copy(one_r[:, :], ones_row[:, :]).then_inc(tgbo_ready, 1)
                for g in groups[EARLY:]:
                    group(*g)

            def step(s, par):
                t = s - LAG
                if active(t):
                    tile = xt[:, ds(t, 1), :].rearrange("p o d -> p (o d)")
                    dve.wait_ge(out_done, t + 1)
                    nc.vector.tensor_tensor(tile, ps[:, 6, D:2 * D], tile, ALU.add).then_inc(x1a_done, 1)
                    dve.wait_ge(x1a_done, t + 1)
                    nc.vector.tensor_tensor(tile, ps[:, 6, 0:D], tile, ALU.add).then_inc(x1_done, 1)
                    dve.wait_ge(x1_done, t + 1)
                    nc.vector.bn_stats(stats2[:, ds(t, 1), :].rearrange("p o s -> p (o s)"), tile).then_inc(stats_done, 1)
                t = s - 2
                if active(t):
                    for half in range(2):
                        dve.wait_ge(phi_ready, 2 * t + half + 1)
                        nc.vector.tensor_tensor(pT_lo[:, par, 4 * half:4 * half + 4, :],
                                                ps[:, 4 + half, :].rearrange("p (m i) -> p m i", m=4),
                                                as_f32(pT_hi[:, par, 4 * half:4 * half + 4, :]),
                                                ALU.subtract).then_inc(plo_ready, 1)
                t = s - 1
                if active(t):
                    q = (par - 1) % 2
                    dve.wait_ge(exp_done, t + 1)
                    nc.vector.tensor_reduce(sm[:, q, 0:H // 2], sx[:, q, 0:BANK].rearrange("p (h m) -> p h m", m=M),
                                            AX, ALU.add).then_inc(sum_done, 1)
                    dve.wait_ge(sum_done, t + 1)
                    dve.wait_ge(head_done, t + 1)
                    wait_pos(dve, mul_done, t - 1)
                    nc.vector.reciprocal(rs[:, q, :], sm[:, q, :]).then_inc(recip_done, 1)
                t = s + 1
                if active(t):
                    q = (par + 1) % 2
                    dve.wait_ge(xhi_ready, t + 1)
                    nc.vector.tensor_tensor(xT_lo[:, q, :, :], ps[:, 7, 0:D].rearrange("p (k i) -> p k i", k=KD),
                                            as_f32(xT_hi[:, q, :, :]), ALU.subtract).then_inc(xlo_ready, 1)
                t = s
                if active(t):
                    dve.wait_ge(scores_done, t + 1)
                    sc = ps[:, 2 * par:2 * par + 2, :].rearrange("p a (h m) -> p (a h) m", m=M)
                    nc.vector.tensor_reduce(mx[:, par, :], sc, AX, ALU.max, negate=True).then_inc(max_done, 1)
                    dve.wait_ge(max_done, t + 1)
                    wait_pos(dve, pT_done, 2 * (t - 1))
                    nc.vector.tensor_tensor(sx[:, par, 0:BANK].rearrange("p (h m) -> p h m", m=M),
                                            sc[:, 0:H // 2, :],
                                            mx[:, par, 0:H // 2].unsqueeze(2).broadcast_to([P, H // 2, M]),
                                            ALU.add).then_inc(sub_done, 1)
            run_steps(dve, step, value_groups)

            dve.wait_ge(stats_done, 2 * NT)
            rstd_from(stats2, mean2, rstd2, 2)
            dve.wait_ge(xT_done, NT)

            def y_tile(t, par):
                if not isinstance(t, int) or t >= 2:
                    dve.wait_ge(yT_done, t - 1)
                nc.vector.tensor_scalar(xn[:, par, :], xt[:, ds(t, 1), :].rearrange("p o d -> p (o d)"),
                                        mean2[:, ds(t, 1)], rstd2[:, ds(t, 1)], ALU.subtract,
                                        ALU.mult).then_inc(y_ready, 1)

            def y_low(t, par):
                dve.wait_ge(yhi_ready, t + 1)
                nc.vector.tensor_tensor(yT_lo[:, :, ds(t * P, P)],
                                        ps[:, 6 + par, 0:D].rearrange("p (k i) -> p k i", k=KD),
                                        as_f32(yT_hi[:, :, ds(t * P, P)]), ALU.subtract).then_inc(ylo_ready, 1)
            y_tile(0, 0)
            y_tile(1, 1)
            with dve.Fori(0, NT // 2 - 1) as i:
                for par in range(2):
                    y_tile(i * 2 + 2 + par, par)
                    y_low(i * 2 + par, par)
            y_low(NT - 2, 0)
            y_low(NT - 1, 1)

            nc.vector.tensor_reduce(rep[:, :, :], ysum[:, :, :].rearrange("p k (b t) -> p k b t", b=B), AX,
                                    ALU.add).then_inc(route_step, 1)
            dve.wait_ge(route_step, 1)
            nc.vector.tensor_scalar(rep[:, :, :], rep[:, :, :], 1.0 / S, None, ALU.mult).then_inc(rep_ready, 1)
            done = [1]

            def link(ins):
                done[0] += 1
                ins.then_inc(route_step, 1)
                dve.wait_ge(route_step, done[0])

            def by_batch(r):
                return row[:, r, :].rearrange("p (b e) -> p b e", b=B)

            dve.wait_ge(logits_done, 1)
            lg = ps[0:1, 0, 0:B * E].rearrange("p (b e) -> p b e", b=B)
            top = row[:, 10, 0:B]
            nc.vector.tensor_reduce(top, lg, AX, ALU.max).then_inc(ln_step, 1)
            dve.wait_ge(ln_step, 15)
            link(nc.vector.tensor_tensor(by_batch(1), lg, top.unsqueeze(2).broadcast_to([1, B, E]), ALU.subtract))
            dve.wait_ge(route_exp, 1)
            link(nc.vector.tensor_reduce(row[:, 11, 0:B], by_batch(2), AX, ALU.add))
            link(nc.vector.reciprocal(row[:, 12, 0:B], row[:, 11, 0:B]))
            link(nc.vector.tensor_tensor(by_batch(3), by_batch(2),
                                         row[:, 12, 0:B].unsqueeze(2).broadcast_to([1, B, E]), ALU.mult))
            for b in range(B):
                nc.vector.max(row[:, 4, b * E:(b + 1) * E], row[:, 3, b * E:(b + 1) * E])
            link(nc.vector.memset(row[:, 5, :], 0.0))
            for b in range(B):
                last = nc.vector.max_index(idx[:, b * E:(b + 1) * E], row[:, 4, b * E:(b + 1) * E],
                                           row[:, 3, b * E:(b + 1) * E])
            link(last)
            link(nc.vector.tensor_copy(row[:, 6, :], idx[:, :]))
            v, ind = by_batch(4), by_batch(6)
            link(nc.vector.tensor_tensor(row[:, 7, 0:B], v[:, :, 0], v[:, :, 1], ALU.add))
            link(nc.vector.reciprocal(row[:, 8, 0:B], row[:, 7, 0:B]))
            link(nc.vector.tensor_tensor(row[:, 9, 0:NQ].rearrange("p (b s) -> p b s", b=B), v[:, :, 0:TOP],
                                         row[:, 8, 0:B].unsqueeze(2).broadcast_to([1, B, TOP]), ALU.mult))
            link(nc.vector.tensor_scalar(row[:, 13, 0:NQ], row[:, 9, 0:NQ], tg[0:1, 1:2], None, ALU.mult))
            dve.wait_ge(rows_ready, 1)
            for b in range(B):
                for slot in range(TOP):
                    q = b * TOP + slot
                    last = nc.vector.tensor_scalar(hot[:, q, :], iota_row[:, :], row[:, 6, b * E + slot:b * E + slot + 1],
                                                   None, ALU.is_equal)
            link(last)
            for b in range(B):
                link(nc.vector.tensor_scalar(hot[:, NQ + b, :], hot[:, b * TOP, :],
                                             row[:, 13, b * TOP:b * TOP + 1], None, ALU.mult))
                last = nc.vector.scalar_tensor_tensor(hot[:, NQ + b, :], hot[:, b * TOP + 1, :],
                                                      row[:, 13, b * TOP + 1:b * TOP + 2], hot[:, NQ + b, :],
                                                      ALU.mult, ALU.add)
            last.then_inc(hot_ready, 1)
            dve.wait_ge(hotT_done, 1)
            nc.vector.tensor_copy(hotT[:, :], ps[0:E, 1, 0:NQ + B]).then_inc(hotT_ready, 1)
            dve.wait_ge(sel_done, 1)
            nc.vector.tensor_copy(b1sel[:, :, :], ps[:, 2, 0:NF * NQ].rearrange("p (f q) -> p f q", q=NQ))
            nc.vector.tensor_copy(b2sel[:, :, :], ps[:, 3, 0:KD * B].rearrange("p (k b) -> p k b", b=B))
            nc.vector.tensor_copy(swt[:, :], ps[:, 3, 64:64 + NQ]).then_inc(sel_ready, 1)
            dve.wait_ge(sel_ready, 1)

            dve.wait_ge(w_hi_done, 1)
            nc.vector.tensor_tensor(w1_lo[0][:, :, :], stage_w1[0][:, :, :], as_f32(w1_hi[0][:, :, :]),
                                    ALU.subtract).then_inc(w_lo_done, 1)
            dve.wait_ge(w_hi_done, 2)
            nc.vector.scalar_tensor_tensor(w2_lo[0][:, :, :], stage_w2[0][:, :, :], swt[:, 0:1],
                                           as_f32(w2_hi[0][:, :, :]), ALU.mult, ALU.subtract).then_inc(w_lo_done, 1)

            dve.sem_inc(hlo_ready, FREE_GELS)
            with dve.Fori(0, B) as b:
                for slot in range(TOP):
                    with dve.Fori(0, NCH) as c:
                        for f in range(NF):
                            n = ((b * TOP + slot) * NCH + c) * NF + f
                            dve.wait_ge(gelu_done, n + 1 + FREE_BANKS)
                            dve.wait_ge(w2_done, n + 1)
                            nc.vector.tensor_copy(h_hi[:, f % 4, :], gel[:, f % 2, :]).then_inc(hhi_ready, 1)
                            dve.wait_ge(hhi_ready, n + 1)
                            nc.vector.tensor_tensor(h_lo[:, f % 4, :], gel[:, f % 2, :], as_f32(h_hi[:, f % 4, :]),
                                                    ALU.subtract).then_inc(hlo_ready, 1)
                            nxt = 1 - slot
                            dve.wait_ge(w_hi_done, n * 2 + 3)
                            nc.vector.tensor_tensor(w1_lo[nxt][:, ds(c, 1), f * P:(f + 1) * P],
                                                    stage_w1[nxt][:, ds(c, 1), f * P:(f + 1) * P],
                                                    as_f32(w1_hi[nxt][:, ds(c, 1), f * P:(f + 1) * P]),
                                                    ALU.subtract).then_inc(w_lo_done, 1)
                            dve.wait_ge(w_hi_done, n * 2 + 4)
                            sc = (b * TOP + slot + 1) if slot == 0 else b * 0 + (NQ // 2)
                            nc.vector.scalar_tensor_tensor(w2_lo[nxt][:, f, ds(c * P, P)],
                                                           stage_w2[nxt][:, f, ds(c * P, P)], swt[:, ds(sc, 1)],
                                                           as_f32(w2_hi[nxt][:, f, ds(c * P, P)]), ALU.mult,
                                                           ALU.subtract).then_inc(w_lo_done, 1)
                for tt in range(TB):
                    t = b * TB + tt
                    tile = xt[:, ds(t, 1), :].rearrange("p o d -> p (o d)")
                    dve.wait_ge(oTT_done, t + 1 + FREE_SUM)
                    nc.vector.tensor_tensor(tile, ps[:, 4 + tt % 4, 0:D], tile, ALU.add).then_inc(x2_done, 1)

        @block.tensor
        def _(pe):
            mm = nc.tensor.matmul
            pe.wait_ge(ident_ready, 1)

            def three(acc, hi_w, lo_w, hi_x, lo_x, start, stop):
                mm(acc, hi_w, hi_x, start=start, stop=False)
                mm(acc, hi_w, lo_x, start=False, stop=False)
                return mm(acc, lo_w, hi_x, start=False, stop=stop)

            def group(kind, i):
                n = number[(kind, i)]
                bank = ps[:, GRP_BANK[(kind, i)], :]
                if GRP_BEFORE[(kind, i)]:
                    wait_group_read(pe, *GRP_BEFORE[(kind, i)])
                if kind == "ctxT":
                    pe.wait_ge(ld_ctx, 16)
                    for k in range(KD):
                        last = nc.tensor.transpose(bank[:, k * P:(k + 1) * P], ctx_sb[:, k * P:(k + 1) * P], ident[:, :])
                if kind in ("kT", "vT"):
                    w_sb = wk_sb if kind == "kT" else wv_sb
                    pe.wait_ge(ld_wk if kind == "kT" else ld_wv, 16)
                    wait_group_read(pe, "ctxT", 0)
                    for m in range(4):
                        for k in range(KD):
                            c0 = (4 * i + m) * P
                            last = mm(bank[:, m * P:(m + 1) * P], w_sb[:, k, c0:c0 + P], ctxT[:, k, :],
                                      start=(k == 0), stop=(k == KD - 1))
                if kind == "wqT":
                    pe.wait_ge(ld_wq, 16)
                    for m in range(2):
                        for k in range(KD):
                            c0 = (2 * i + m) * P
                            last = nc.tensor.transpose(bank[:, (m * KD + k) * P:(m * KD + k + 1) * P],
                                                       wq_sb[:, k, c0:c0 + P], ident[:, :])
                if kind == "A":
                    ct, mp = i // 4, i % 4
                    wait_group_read(pe, "kT", mp // 2)
                    wait_group_read(pe, "wqT", mp)
                    for m in range(2):
                        last = mm(bank[:, m * B * P:(m + 1) * B * P], wqT[:, 2 * mp + m, ct * P:(ct + 1) * P],
                                  kbd[:, 2 * mp + m, :, :].rearrange("p b x -> p (b x)"), start=True, stop=True)
                if kind == "VW":
                    b, mp = i // 4, i % 4
                    pe.wait_ge(ld_wo, 16)
                    wait_group_read(pe, "vT", mp // 2)
                    for m in range(2):
                        last = mm(bank[:, m * D:(m + 1) * D], vbd[:, 2 * mp + m, b, :], wo_sb[:, 2 * mp + m, :],
                                  start=True, stop=True)
                last.then_inc(grp_done, 1)
            for g in groups[:EARLY]:
                group(*g)
            wait_group_read(pe, "A", 7)

            def value_groups():
                for g in groups[EARLY:]:
                    group(*g)

            def step(s, par):
                t = s - 2
                if active(t):
                    pe.wait_ge(mul_done, t + 1)
                    for half in range(2):
                        wait_pos(pe, plo_ready, 2 * t + half - 1)
                        for m in range(4):
                            c0 = (4 * half + m) * P
                            last = nc.tensor.transpose(ps[:, 4 + half, m * P:(m + 1) * P],
                                                       sx[:, par, c0:c0 + P], ident[:, :])
                        last.then_inc(pT_done, 1)
                t = s + 1
                if active(t):
                    q = (par + 1) % 2
                    pe.wait_ge(xn_ready, t + 1)
                    wait_pos(pe, xlo_ready, t)
                    for k in range(KD):
                        last = nc.tensor.transpose(ps[:, 7, k * P:(k + 1) * P], xn[:, q, k * P:(k + 1) * P], ident[:, :])
                    last.then_inc(xT_done, 1)
                t = s
                if active(t):
                    pe.wait_ge(xlo_ready, t + 1)
                    wait_pos(pe, sub_done, t - 1)
                    wait_pos(pe, head_done, t - 1)
                    boff = (t // TB) * HM
                    for c in range(2):
                        for k in range(KD):
                            lo, hi = xT_lo[:, par, k, :], xT_hi[:, par, k, :]
                            wh, wl = (w[:, k, ds(boff + c * BANK, BANK)] for w in (a_hi, a_lo))
                            last = three(ps[:, 2 * par + c, :], hi, lo, wh, wl, k == 0, k == KD - 1)
                    last.then_inc(scores_done, 1)
                t = s - 2
                if active(t):
                    wait_pos(pe, x1_done, t)
                    bm = (t // TB) * NP
                    if isinstance(t, int) and t == 0:
                        pe.wait_ge(tgbo_ready, 3)
                    mm(ps[:, 6, :], one_r[:, :], bo_parts[:, :], start=True, stop=False)
                    for m in range(NP):
                        if m % 4 == 0:
                            pe.wait_ge(plo_ready, 2 * t + m // 4 + 1)
                        mm(ps[:, 6, :], pT_hi[:, par, m, :], vw[:, ds(bm + m, 1), :].rearrange("p o n -> p (o n)"),
                           start=False, stop=False)
                        last = mm(ps[:, 6, 0:D], pT_lo[:, par, m, :],
                                  vw[:, ds(bm + m, 1), 0:D].rearrange("p o n -> p (o n)"),
                                  start=False, stop=(m == NP - 1))
                    last.then_inc(out_done, 1)
            run_steps(pe, step, value_groups)

            pe.wait_ge(x1_done, NT)
            pe.wait_ge(xlo_ready, NT)

            def y_transpose(t, par):
                pe.wait_ge(y_ready, t + 1)
                if not isinstance(t, int) or t >= 2:
                    pe.wait_ge(ylo_ready, t - 1)
                for k in range(KD):
                    last = nc.tensor.transpose(ps[:, 6 + par, k * P:(k + 1) * P], xn[:, par, k * P:(k + 1) * P],
                                               ident[:, :])
                last.then_inc(yT_done, 1)
            y_transpose(0, 0)
            y_transpose(1, 1)
            with pe.Fori(1, NT // 2) as i:
                y_transpose(i * 2, 0)
                y_transpose(i * 2 + 1, 1)

            pe.wait_ge(rep_ready, 1)
            pe.wait_ge(sub_done, NT)
            pe.wait_ge(head_done, NT)
            for b in range(B):
                for k in range(KD):
                    last = mm(ps[0:1, 0, b * E:(b + 1) * E], rep[:, k, b:b + 1], gate_sb[:, k, :],
                              start=(k == 0), stop=(k == KD - 1))
            last.then_inc(logits_done, 1)
            pe.wait_ge(hot_ready, 1)
            for r in range(NQ + B):
                last = mm(ps[0:E, 1, r:r + 1], hot[:, r, :], ones_row[0:1, 0:1], start=True, stop=True)
            last.then_inc(hotT_done, 1)
            pe.wait_ge(hotT_ready, 1)
            pe.wait_ge(ld_b12, 32)
            for f in range(NF):
                mm(ps[:, 2, f * NQ:(f + 1) * NQ], b1_sb[:, f * P:(f + 1) * P], hotT[:, 0:NQ], start=True, stop=True)
            for k in range(KD):
                mm(ps[:, 3, k * B:(k + 1) * B], b2_sb[:, k * P:(k + 1) * P], hotT[:, NQ:NQ + B], start=True, stop=True)
            mm(ps[:, 3, 64:64 + NQ], ones_row[:, :], row[:, 13, 0:NQ], start=True, stop=True).then_inc(sel_done, 1)
            pe.wait_ge(sel_ready, 1)
            pe.wait_ge(ylo_ready, NT)
            pe.sem_inc(w2_done, FREE_SPLITS)
            pe.sem_inc(oTT_done, FREE_SUM)

            def first_layer(slot, c, f, b):
                n = ((b * TOP + slot) * NCH + c) * NF + f
                tok = (b * NCH + c) * CH
                pe.wait_ge(gelu_done, n + 1)
                for k in range(KD):
                    hi, lo = (w[slot][:, k, f * P:(f + 1) * P] for w in (w1_hi, w1_lo))
                    last = three(ps[:, 4 + f % 4, :], hi, lo, yT_hi[:, k, ds(tok, CH)], yT_lo[:, k, ds(tok, CH)],
                                 k == 0, k == KD - 1)
                last.then_inc(h_done, 1)

            def second_layer(slot, c, f, b):
                n = ((b * TOP + slot) * NCH + c) * NF + f
                pe.wait_ge(hlo_ready, n + 1 + FREE_GELS)
                for d in range(KD):
                    hi, lo = (w[slot][:, f, d * P:(d + 1) * P] for w in (w2_hi, w2_lo))
                    acc = ps[:, ds(c * KD + d, 1), :].rearrange("p o n -> p (o n)")
                    last = three(acc, hi, lo, h_hi[:, f % 4, :], h_lo[:, f % 4, :],
                                 slot == 0 and f == 0, slot == TOP - 1 and f == NF - 1)
                last.then_inc(w2_done, 1)

            with pe.Fori(0, B) as b:
                for slot in range(TOP):
                    with pe.Fori(0, NCH) as c:
                        pe.wait_ge(w_lo_done, (b * TOP + slot) * (2 * NCH * NF) + 2)
                        for f in range(NF):
                            first_layer(slot, c, f, b)
                            if f >= 2:
                                second_layer(slot, c, f - 2, b)
                        second_layer(slot, c, NF - 2, b)
                        second_layer(slot, c, NF - 1, b)
                for tt in range(TB):
                    pe.wait_ge(oT_ready, b * NCH * KD + (2 if tt < TB // 2 else 4))
                    if tt >= 4:
                        pe.wait_ge(x2_done, b * TB + tt - 3)
                    for d in range(KD):
                        last = nc.tensor.transpose(ps[:, 4 + tt % 4, d * P:(d + 1) * P],
                                                   oT[:, d, tt * P:(tt + 1) * P], ident[:, :])
                    last.then_inc(oTT_done, 1)
                pe.wait_ge(x2_done, (b + 1) * TB)


_INS = ["x", "ctx_1024", "g_xattn", "g_ffn", "L0_xattn_Wq", "L0_xattn_Wk", "L0_xattn_Wv", "L0_xattn_Wo",
        "L0_xattn_bo", "L0_ffn_gate_w", "L0_ffn_w1", "L0_ffn_b1", "L0_ffn_w2", "L0_ffn_b2"]


def kernel(**inputs):
    import numpy as _np
    import concourse.bacc as _bacc
    from concourse import mybir as _mybir
    from concourse.bass_utils import run_bass_kernel_spmd as _run

    nc = _bacc.Bacc("TRN2", target_bir_lowering=False, num_devices=1)
    arrays, args = {}, []
    for name in _INS:
        a = _np.ascontiguousarray(inputs[name])
        arrays[f"in_{name}_dram"] = a
        args.append(nc.dram_tensor(f"in_{name}_dram", a.shape, _mybir.dt.from_np(a.dtype), kind="ExternalInput").ap())
    shape = inputs["x"].shape
    out = nc.dram_tensor("out_0_dram", (shape[0] * shape[1], shape[2]), _mybir.dt.float32,
                         kind="ExternalOutput").ap()
    gated_cross_attention_moe_kernel(nc, *args, out)
    r = _run(nc, [arrays], core_ids=[0])
    return r.results[0]["out_0_dram"].reshape(shape)
```

```python
import concourse.bass as bass
from concourse import mybir
from contextlib import ExitStack


def gated_cross_attention_moe_kernel(nc, x, ctx_tokens, g_xattn, g_ffn, Wq, Wk, Wv, Wo, bo,
                                     gate_w, w1, b1, w2, b2, out):
    f32 = mybir.dt.float32
    f32r = mybir.dt.float32r
    u32 = mybir.dt.uint32
    i32 = mybir.dt.int32
    ALU = mybir.AluOpType
    ACT = mybir.ActivationFunctionType
    AX = mybir.AxisListType.X
    ds = bass.ds

    P = 128
    B, S, D = x.shape
    M = ctx_tokens.shape[1]
    HD = Wq.shape[1]
    DH = 64
    H = HD // DH
    E, _, F = w1.shape
    TOP = 2
    NT = B * S // P
    TB = S // P
    KD = D // P
    NP = HD // P
    NF = F // P
    HM = H * M
    CH = 512
    NCH = S // CH
    BANK = 512
    NQ = B * TOP
    SCALE = DH ** -0.5
    EPS = 1e-5
    LEAD, LAG = 2, 3
    assert 2 * DH == P and 2 * M == P and B * M == P and TOP == 2 and NCH == 2 and KD == 2

    xf = x.rearrange("b s d -> (b s) d")

    cursor = [(nc.sbuf_base + 63) // 64 * 64]

    def place(name, shape, dtype=f32, at=None):
        size = 4
        for n in shape[1:]:
            size *= n
        offset = cursor[0] if at is None else at[0]
        t = nc.alloc_sbuf_tensor_at(name, shape, dtype, offset=offset)
        (cursor if at is None else at)[0] = offset + (size + 31) // 32 * 32
        return t

    xt = place("xt", [P, NT, D])
    yT_hi = place("yT_hi", [P, KD, NT * P], f32r)
    yT_lo = place("yT_lo", [P, KD, NT * P], f32r)
    ident = place("ident", [P, P])
    gate_sb = place("gate_sb", [P, KD, E])
    stats1 = place("stats1", [P, NT, 6])
    stats2 = stats1
    mean1 = place("mean1", [P, NT])
    rstd1 = place("rstd1", [P, NT])
    mean2 = place("mean2", [P, NT])
    rstd2 = place("rstd2", [P, NT])
    ve = place("ve", [P, TB])
    dm = place("dm", [P, TB])
    nu = place("nu", [P, TB])
    half_bits = place("half_bits", [P, TB], i32)
    gg = place("gg", [P, 2])
    tg = place("tg", [P, 2])
    mx = place("mx", [P, 2, H])
    sm = place("sm", [P, 2, H])
    rs = place("rs", [P, 2, H])
    ysum = place("ysum", [P, KD, NT])
    rep = place("rep", [P, KD, B])
    row = place("row", [1, 16, E])
    idx = place("idx", [1, B, E], u32)
    hot = place("hot", [1, TOP + 1, E])
    hotT = place("hotT", [E, TOP + 1])
    ones_row = place("ones_row", [1, P])
    iota_row = place("iota_row", [1, E])
    b1sel = place("b1sel", [P, B, NF, TOP])
    b2sel = place("b2sel", [P, B, KD])
    swt = place("swt", [P, NQ])
    bo_row = place("bo_row", [1, D])
    bo_parts = place("bo_parts", [1, 2 * D], f32r)
    one_r = place("one_r", [1, P], f32r)

    first = [cursor[0]]
    wq_sb = place("wq_sb", [P, KD, HD], at=first)
    wk_sb = place("wk_sb", [P, KD, HD], at=first)
    wv_sb = place("wv_sb", [P, KD, HD], at=first)
    wo_sb = place("wo_sb", [P, NP, D], at=first)
    wqT = place("wqT", [P, NP, D], at=first)
    kbd = place("kbd", [P, NP, B, P], at=first)
    vbd = place("vbd", [P, NP, B, P], at=first)
    ctx_sb = place("ctx_sb", [P, D], at=first)
    ctxT = place("ctxT", [P, KD, P], at=first)
    first2 = [cursor[0]]
    stage_w1 = [place("stage_w1_0", [P, KD, F], at=first2)]
    stage_w2 = [place("stage_w2_0", [P, NF, D], at=first2)]
    w1_hi = [place("w1_hi_0", [P, KD, F], f32r, at=first2)]
    w1_lo = [place("w1_lo_0", [P, KD, F], f32r, at=first2)]
    w2_hi = [place("w2_hi_0", [P, NF, D], f32r, at=first2)]
    w2_lo = [place("w2_lo_0", [P, NF, D], f32r, at=first2)]
    first3 = [first2[0]]
    oT = place("oT", [P, KD, S], at=first2)
    b1_sb = place("b1_sb", [E, F], at=first3)
    b2_sb = place("b2_sb", [E, D], at=first3)
    yb = place("yb", [P, 2, D], at=first3)
    assert first3[0] <= first2[0]

    second = [max(first[0], first2[0])]
    second2 = [second[0]]
    a_hi = place("a_hi", [P, KD, B * HM], f32r, at=second)
    a_lo = place("a_lo", [P, KD, B * HM], f32r, at=second)
    vw = place("vw", [P, B * NP, 2 * D], f32r, at=second)
    sx = place("sx", [P, 2, HM], at=second)
    third = [second[0]]
    pT_hi = place("pT_hi", [P, 2, NP, P], f32r, at=second)
    pT_lo = place("pT_lo", [P, 2, NP, P], f32r, at=second)
    xT_hi = place("xT_hi", [P, 2, KD, P], f32r, at=second)
    xT_lo = place("xT_lo", [P, 2, KD, P], f32r, at=second)
    xn = place("xn", [P, 2, D], at=second)
    stage_w1.append(place("stage_w1_1", [P, KD, F], at=second2))
    stage_w2.append(place("stage_w2_1", [P, NF, D], at=second2))
    w1_hi.append(place("w1_hi_1", [P, KD, F], f32r, at=second2))
    w1_lo.append(place("w1_lo_1", [P, KD, F], f32r, at=second2))
    w2_hi.append(place("w2_hi_1", [P, NF, D], f32r, at=second2))
    w2_lo.append(place("w2_lo_1", [P, NF, D], f32r, at=second2))
    gel = place("gel", [P, 2, CH], at=second2)
    h_hi = place("h_hi", [P, 4, CH], f32r, at=second2)
    h_lo = place("h_lo", [P, 4, CH], f32r, at=third)
    assert second2[0] <= third[0] and third[0] <= second[0]

    def as_f32(ap):
        return ap.bitcast(f32)

    stack = ExitStack()
    with stack:
        ps = stack.enter_context(nc.psum_tensor("ps", [P, 8, BANK], f32))

        def sem(name):
            return stack.enter_context(nc.semaphore(name))

        ld_ctx, ld_wk, ld_wq, ld_wv, ld_wo = (sem("ld_" + n) for n in ("ctx", "wk", "wq", "wv", "wo"))
        ld_x = [sem(f"ld_x_{b}") for b in range(B)]
        ld_small, ld_b12 = sem("ld_small"), sem("ld_b12")
        ident_ready, zeros_ready, rows_ready = sem("ident_ready"), sem("zeros_ready"), sem("rows_ready")
        tanh_done, tgbo_ready = sem("tanh_done"), sem("tgbo_ready")
        grp_done, grp_act, grp_dve = sem("grp_done"), sem("grp_act"), sem("grp_dve")
        grp_hi = sem("grp_hi")
        stats_done, ln_step = sem("stats_done"), sem("ln_step")
        ln_ready, xc_ready = sem("ln_ready"), sem("xc_ready")
        xn_ready, xT_done, xhi_ready, xlo_ready = (
            sem(n) for n in ("xn_ready", "xT_done", "xhi_ready", "xlo_ready"))
        scores_done, head_done, max_done, sub_done, exp_done, sum_done, recip_done, mul_done = (
            sem(n) for n in ("scores_done", "head_done", "max_done", "sub_done", "exp_done", "sum_done",
                             "recip_done", "mul_done"))
        pT_done, phi_ready, plo_ready, out_done, x1a_done, x1_done = (
            sem(n) for n in ("pT_done", "phi_ready", "plo_ready", "out_done", "x1a_done", "x1_done"))
        y_ready, yT_done, yhi_ready, ylo_ready = (
            sem(n) for n in ("y_ready", "yT_done", "yhi_ready", "ylo_ready"))
        rep_ready, logits_done, route_step, route_sub, route_exp, idx_ready, hot_ready, hotT_done, hotT_ready, sel_done, sel_ready = (
            sem(n) for n in ("rep_ready", "logits_done", "route_step", "route_sub", "route_exp", "idx_ready", "hot_ready",
                             "hotT_done", "hotT_ready", "sel_done", "sel_ready"))
        staged = [sem("staged_0"), sem("staged_1")]
        w_hi_done, w_lo_done = sem("w_hi_done"), sem("w_lo_done")
        h_done, gelu_done, hhi_ready, hlo_ready, w2_done = (
            sem(n) for n in ("h_done", "gelu_done", "hhi_ready", "hlo_ready", "w2_done"))
        FREE_BANKS, FREE_GELS, FREE_SPLITS = 2, 2, 4
        oT_ready, oTT_done, x2_done, stored = (
            sem(n) for n in ("oT_ready", "oTT_done", "x2_done", "stored"))

        groups = ([("ctxT", 0)] + [("kT", i) for i in range(2)] + [("wqT", i) for i in range(4)]
                  + [("A", i) for i in range(8)] + [("vT", i) for i in range(2)]
                  + [("VW", i) for i in range(8)])
        number = {g: n for n, g in enumerate(groups)}
        EARLY = number[("vT", 0)]
        GRP_BANK = {g: n % 8 if n < EARLY else 4 + (n - EARLY) % 3 for n, g in enumerate(groups)}
        GRP_BEFORE = {g: next((h for h in reversed(groups[:n]) if GRP_BANK[h] == GRP_BANK[g]), None)
                      for n, g in enumerate(groups)}
        reader = {}
        counts = {"act": 0, "dve": 0}
        for kind, i in groups:
            who = "act" if kind in ("kT", "wqT", "vT") and i % 2 == 0 else "dve"
            counts[who] += 1
            reader[(kind, i)] = (who, counts[who])

        def wait_group_read(eng, kind, i):
            who, n = reader[(kind, i)]
            eng.wait_ge(grp_act if who == "act" else grp_dve, n)

        LOGITS = [0, 6]
        STEPS = list(range(-LEAD, NT + LAG))
        Y_FROM = TB + LAG + 1
        ROUTE_AT = Y_FROM + TB // 2
        LOOP0, LOOP1 = LAG + 1, Y_FROM
        assert (LOOP1 - LOOP0) % 2 == 0 and ROUTE_AT == NT

        def run_steps(eng, step, value_groups=lambda: None, norm_begins=lambda: None, route=lambda: None):
            for s in STEPS:
                if s == 1:
                    value_groups()
                if s < LOOP0:
                    step(s, s % 2)
            with eng.Fori(0, (LOOP1 - LOOP0) // 2) as i:
                step(LOOP0 + i * 2, 0)
                step(LOOP0 + 1 + i * 2, 1)
            for s in STEPS:
                if s >= LOOP1:
                    if s == Y_FROM:
                        norm_begins()
                    if s == ROUTE_AT:
                        route()
                    step(s, s % 2)

        def norm_tiles(s):
            return range(2 * (s - Y_FROM), 2 * (s - Y_FROM) + 2) if isinstance(s, int) and Y_FROM <= s < ROUTE_AT else ()

        def active(t):
            return not isinstance(t, int) or 0 <= t < NT

        def wait_pos(eng, s, v):
            if not isinstance(v, int) or v > 0:
                eng.wait_ge(s, v)

        block = stack.enter_context(nc.Block())

        @block.sync
        def _(sp):
            def load_x(b):
                sp.dma_start(xt[:, b * TB:(b + 1) * TB, :],
                             xf[b * S:(b + 1) * S, :].rearrange("(t p) d -> p t d", p=P)).then_inc(ld_x[b], 16)

            sp.dma_start(ctx_sb[:, :], ctx_tokens.rearrange("b m d -> (b m) d")).then_inc(ld_ctx, 16)
            sp.dma_start(wk_sb[:, :, :], Wk.rearrange("(k p) n -> p k n", p=P)).then_inc(ld_wk, 16)
            sp.dma_start(wq_sb[:, :, :], Wq.rearrange("(k p) n -> p k n", p=P)).then_inc(ld_wq, 16)
            load_x(0)
            sp.dma_start(wv_sb[:, :, :], Wv.rearrange("(k p) n -> p k n", p=P)).then_inc(ld_wv, 16)
            sp.dma_start(wo_sb[:, :, :], Wo.rearrange("(k p) n -> p k n", p=P)).then_inc(ld_wo, 16)
            load_x(1)

            sp.wait_ge(grp_done, len(groups))
            sp.dma_start(b1_sb[:, :], b1).then_inc(ld_b12, 16)
            sp.dma_start(b2_sb[:, :], b2).then_inc(ld_b12, 16)

            for q in range(NQ):
                b, slot = q // TOP, q % TOP
                if q < TOP:
                    sp.wait_ge(*((x1_done, 1) if slot == 0 else (out_done, NT)))
                else:
                    sp.wait_ge(w_lo_done, 2 + 2 * NCH * NF * (q - TOP))
                sp.wait_ge(idx_ready, b + 1)
                e = sp.value_load(idx[0:1, b, slot:slot + 1], min_val=0, max_val=E - 1)
                sp.dma_start(stage_w1[slot][:, :, :],
                             w1[ds(e, 1), :, :].rearrange("o (k p) n -> p (o k) n", p=P)).then_inc(staged[slot], 16)
                sp.dma_start(stage_w2[slot][:, :, :],
                             w2[ds(e, 1), :, :].rearrange("o (k p) n -> p (o k) n", p=P)).then_inc(staged[slot], 16)

            with sp.Fori(0, NT // 2) as i:
                sp.wait_ge(x2_done, i + 1)
                sp.dma_start(out[ds(i * 2 * P, 2 * P), :].rearrange("(t p) d -> p t d", p=P),
                             xt[:, ds(i * 2, 2), :]).then_inc(stored, 16)
            sp.wait_ge(stored, 16 * (NT // 2))

        @block.gpsimd
        def _(pool):
            nc.gpsimd.memset(ident[:, :], 0.0).then_inc(zeros_ready, 1)
            pool.wait_ge(zeros_ready, 1)
            nc.gpsimd.affine_select(out=ident[:, :], in_=ident[:, :], compare_op=ALU.not_equal, fill=1.0,
                                    base=0, pattern=[[-1, P]], channel_multiplier=1).then_inc(ident_ready, 1)
            nc.gpsimd.memset(kbd[:, :, :, :], 0.0).then_inc(zeros_ready, 1)
            nc.gpsimd.memset(vbd[:, :, :, :], 0.0).then_inc(zeros_ready, 1)
            nc.gpsimd.memset(ones_row[:, :], 1.0)
            for e in range(E):
                last = nc.gpsimd.memset(iota_row[:, e:e + 1], float(e))
            last.then_inc(rows_ready, 1)

            def step(s, par):
                t = s - 1
                if active(t):
                    q = (par - 1) % 2
                    pool.wait_ge(recip_done, t + 1)
                    pr = sx[:, q, :].rearrange("p (h m) -> p h m", m=M)
                    nc.gpsimd.tensor_tensor(pr, pr, rs[:, q, :].unsqueeze(2).broadcast_to([P, H, M]),
                                            ALU.mult).then_inc(mul_done, 1)
                t = s + LEAD
                if active(t):
                    wait_pos(pool, xT_done, t - 1)
                    tile = xt[:, ds(t, 1), :].rearrange("p o d -> p (o d)")
                    nc.gpsimd.tensor_tensor(xn[:, par, :], tile, mean1[:, ds(t, 1)].broadcast_to([P, D]),
                                            ALU.subtract).then_inc(xc_ready, 1)
                    pool.wait_ge(xc_ready, t + 1)
                    nc.gpsimd.tensor_tensor(xn[:, par, :], xn[:, par, :], rstd1[:, ds(t, 1)].broadcast_to([P, D]),
                                            ALU.mult).then_inc(xn_ready, 1)
            pool.wait_ge(ln_ready, 1)
            run_steps(pool, step)

        @block.scalar
        def _(act):
            act.dma_start(gg[:, 0:1], g_xattn.rearrange("(o n) -> o n", o=1).broadcast_to([P, 1])).then_inc(ld_small, 16)
            act.dma_start(gg[:, 1:2], g_ffn.rearrange("(o n) -> o n", o=1).broadcast_to([P, 1])).then_inc(ld_small, 16)
            act.dma_start(bo_row[:, :], bo.rearrange("(o n) -> o n", o=1)).then_inc(ld_small, 16)
            act.dma_start(gate_sb[:, :, :], gate_w.rearrange("(k p) e -> p k e", p=P)).then_inc(ld_small, 16)

            def y_high(t, bank, c0, until):
                act.wait_ge(yT_done, until)
                for k in range(KD):
                    last = nc.scalar.activation(yT_hi[:, k, t * P:(t + 1) * P],
                                                ps[:, bank, c0 + k * P:c0 + (k + 1) * P],
                                                ACT.Copy, accum_out=ysum[:, k, t:t + 1])
                last.then_inc(yhi_ready, 1)

            def route(b):
                act.wait_ge(route_sub, b + 1)
                nc.scalar.activation(row[:, 2, :], row[:, 1, :], ACT.Exp).then_inc(route_exp, 1)

            def group(kind, i):
                n = number[(kind, i)]
                bank = ps[:, GRP_BANK[(kind, i)], :]
                if kind in ("kT", "vT") and i % 2 == 0:
                    act.wait_ge(grp_done, n + 1)
                    act.wait_ge(zeros_ready, 3)
                    dst = kbd if kind == "kT" else vbd
                    for h in range(2):
                        r = slice(h * DH, (h + 1) * DH)
                        last = nc.scalar.activation(
                            dst[r, 4 * i:4 * i + 4, :, h * M:(h + 1) * M],
                            bank[r, :].rearrange("p (m b j) -> p m b j", m=4, b=B), ACT.Copy,
                            scale=SCALE if kind == "kT" else 1.0)
                    last.then_inc(grp_act, 1)
                if kind == "wqT" and i % 2 == 0:
                    act.wait_ge(grp_done, n + 1)
                    nc.scalar.activation(wqT[:, 2 * i:2 * i + 2, :],
                                         bank.rearrange("p (m c) -> p m c", m=2), ACT.Copy).then_inc(grp_act, 1)
                if kind == "A":
                    act.wait_ge(grp_done, n + 1)
                    ct, mp = i // 4, i % 4
                    dst = a_hi[:, ct, :].rearrange("p (b m x) -> p m b x", b=B, x=P)[:, 2 * mp:2 * mp + 2, :, :]
                    nc.scalar.activation(dst, bank.rearrange("p (m b x) -> p m b x", m=2, b=B),
                                         ACT.Copy).then_inc(grp_hi, 1)
                if kind == "VW":
                    act.wait_ge(grp_done, n + 1)
                    nc.scalar.activation(vw[:, 2 * i:2 * i + 2, 0:D], bank.rearrange("p (m n) -> p m n", m=2),
                                         ACT.Copy, scale=tg[:, 0:1]).then_inc(grp_hi, 1)

            for g in groups[:EARLY]:
                group(*g)
            act.wait_ge(ld_small, 64)
            nc.scalar.activation(tg[:, :], gg[:, :], ACT.Tanh).then_inc(tanh_done, 1)

            def value_groups():
                act.wait_ge(tanh_done, 1)
                for g in groups[EARLY:]:
                    group(*g)

            def step(s, par):
                t = s - 2
                if active(t):
                    for half in range(2):
                        act.wait_ge(pT_done, 2 * t + half + 1)
                        if half == 0:
                            wait_pos(act, out_done, t - 1)
                        nc.scalar.activation(pT_hi[:, par, 4 * half:4 * half + 4, :],
                                             ps[:, 4 + half, :].rearrange("p (m i) -> p m i", m=4),
                                             ACT.Copy).then_inc(phi_ready, 1)
                for y in norm_tiles(s):
                    y_high(y, 7, y % 2 * D, norm_tiles(s)[-1] + 1)
                t = s - 1
                if active(t):
                    q = (par - 1) % 2
                    act.wait_ge(sub_done, t + 1)
                    nc.scalar.activation(sx[:, q, 0:BANK], sx[:, q, 0:BANK], ACT.Exp).then_inc(exp_done, 1)
                t = s + 1
                if active(t):
                    q = (par + 1) % 2
                    act.wait_ge(xT_done, t + 1)
                    wait_pos(act, scores_done, t - 1)
                    nc.scalar.activation(xT_hi[:, q, :, :], ps[:, 7, 0:D].rearrange("p (k i) -> p k i", k=KD),
                                         ACT.Copy).then_inc(xhi_ready, 1)
                t = s
                if active(t):
                    act.wait_ge(max_done, t + 1)
                    wait_pos(act, pT_done, 2 * (t - 1))
                    for h in range(H // 2, H):
                        c0 = h * M
                        last = nc.scalar.activation(sx[:, par, c0:c0 + M], ps[:, 2 * par + 1, c0 - BANK:c0 - BANK + M],
                                                    ACT.Exp, bias=mx[:, par, h:h + 1],
                                                    accum_out=sm[:, par, h:h + 1])
                    last.then_inc(head_done, 1)
            run_steps(act, step, value_groups, route=lambda: route(0))

            act.wait_ge(staged[0], 32)
            act.wait_ge(sel_ready, 1)
            nc.scalar.activation(w1_hi[0][:, :, :], stage_w1[0][:, :, :], ACT.Copy).then_inc(w_hi_done, 1)
            nc.scalar.activation(w2_hi[0][:, :, :], stage_w2[0][:, :, :], ACT.Copy,
                                 scale=swt[:, 0:1]).then_inc(w_hi_done, 1)
            for t in range(TB, NT):
                y_high(t, 6 + t % 2, 0, t + 1)
            route(1)

            def finish(b, chunks):
                act.wait_ge(w2_done, (b + 1) * TOP * NCH * NF + FREE_SPLITS)
                for c in chunks:
                    if b > 0:
                        act.wait_ge(oTT_done, (b - 1) * (TB // 2) + (c + 1) * (TB // 2 // NCH))
                    for d in range(KD):
                        nc.scalar.activation(oT[:, d, c * CH:(c + 1) * CH], ps[:, 2 * c + d, :], ACT.Identity,
                                             bias=b2sel[:, b, d:d + 1]).then_inc(oT_ready, 1)

            act.sem_inc(gelu_done, FREE_BANKS)
            for q in range(NQ):
                b, slot = q // TOP, q % TOP
                if slot == 0 and b > 0:
                    finish(b - 1, range(NCH))
                if slot == TOP - 1 and b + 1 < B:
                    act.wait_ge(sel_ready, b + 2)
                with act.Fori(0, NCH) as c:
                    for f in range(NF):
                        n = (c + q * NCH) * NF + f
                        act.wait_ge(h_done, n + 1)
                        act.wait_ge(hlo_ready, n + 1)
                        nc.scalar.activation(gel[:, f % 2, :], ps[:, 4 + f % 2, :], ACT.Gelu,
                                             bias=b1sel[:, b, f, slot:slot + 1]).then_inc(gelu_done, 1)
                        if q + 1 < NQ:
                            nxt = 1 - slot
                            if f == 0:
                                act.wait_ge(w2_done, q * NCH * NF + FREE_SPLITS)
                                act.wait_ge(staged[nxt], ((q + 1) // TOP + 1) * 32)
                            nc.scalar.activation(w1_hi[nxt][:, ds(c, 1), f * P:(f + 1) * P],
                                                 stage_w1[nxt][:, ds(c, 1), f * P:(f + 1) * P],
                                                 ACT.Copy).then_inc(w_hi_done, 1)
                            nc.scalar.activation(w2_hi[nxt][:, f, ds(c * P, P)], stage_w2[nxt][:, f, ds(c * P, P)],
                                                 ACT.Copy, scale=swt[:, q + 1:q + 2]).then_inc(w_hi_done, 1)
            finish(B - 1, range(NCH))

        @block.vector
        def _(dve):
            ln = [0]

            def link(ins):
                ln[0] += 1
                ins.then_inc(ln_step, 1)
                dve.wait_ge(ln_step, ln[0])

            def norm(b, mean, rstd):
                tiles = slice(b * TB, (b + 1) * TB)
                me, ce, mo, co = (stats1[:, tiles, i] for i in (1, 2, 4, 5))
                m, r = mean[:, tiles], rstd[:, tiles]
                tt, ts, stt = nc.vector.tensor_tensor, nc.vector.tensor_scalar, nc.vector.scalar_tensor_tensor
                tt(dm[:, :], me, mo, ALU.subtract)
                tt(m, me, mo, ALU.add)
                link(tt(ve[:, :], ce, co, ALU.add))
                ts(m, m, 0.5, None, ALU.mult)
                tt(dm[:, :], dm[:, :], dm[:, :], ALU.mult)
                link(ts(ve[:, :], ve[:, :], 1.0 / D, EPS, ALU.mult, ALU.add))
                link(stt(ve[:, :], dm[:, :], 0.25, ve[:, :], ALU.mult, ALU.add))
                link(ts(half_bits[:, :], ve[:, :].bitcast(i32), 1, None, ALU.arith_shift_right))
                link(ts(r.bitcast(i32), half_bits[:, :], -1.0, float(0x5F3759DF), ALU.mult, ALU.add))
                for _ in range(3):
                    link(stt(nu[:, :], ve[:, :], -0.5, r, ALU.mult, ALU.mult))
                    link(tt(nu[:, :], nu[:, :], r, ALU.mult))
                    link(stt(r, nu[:, :], 1.5, r, ALU.add, ALU.mult))

            def x_stats(b):
                dve.wait_ge(ld_x[b], 16)
                with dve.Fori(0, TB // 4) as i:
                    for j in range(4):
                        t = i * 4 + (b * TB + j)
                        nc.vector.bn_stats(stats1[:, ds(t, 1), :].rearrange("p o s -> p (o s)"),
                                           xt[:, ds(t, 1), :].rearrange("p o d -> p (o d)")).then_inc(stats_done, 1)
                dve.wait_ge(stats_done, (b + 1) * TB)
                norm(b, mean1, rstd1)
                dve.sem_inc(ln_ready, 1)

            def group(kind, i):
                n = number[(kind, i)]
                bank = ps[:, GRP_BANK[(kind, i)], :]
                if kind == "ctxT":
                    dve.wait_ge(grp_done, n + 1)
                    nc.vector.tensor_copy(ctxT[:, :, :], bank[:, 0:D].rearrange("p (k i) -> p k i", k=KD)).then_inc(grp_dve, 1)
                if kind in ("kT", "vT") and i % 2 == 1:
                    dve.wait_ge(grp_done, n + 1)
                    dve.wait_ge(zeros_ready, 3)
                    dst = kbd if kind == "kT" else vbd
                    for h in range(2):
                        r = slice(h * DH, (h + 1) * DH)
                        last = nc.vector.tensor_scalar(
                            dst[r, 4 * i:4 * i + 4, :, h * M:(h + 1) * M],
                            bank[r, :].rearrange("p (m b j) -> p m b j", m=4, b=B),
                            SCALE if kind == "kT" else 1.0, None, ALU.mult)
                    last.then_inc(grp_dve, 1)
                if kind == "wqT" and i % 2 == 1:
                    dve.wait_ge(grp_done, n + 1)
                    nc.vector.tensor_copy(wqT[:, 2 * i:2 * i + 2, :],
                                          bank.rearrange("p (m c) -> p m c", m=2)).then_inc(grp_dve, 1)
                if kind == "A" and i == 3:
                    x_stats(0)
                if kind == "A":
                    ct, mp = i // 4, i % 4
                    view = [w[:, ct, :].rearrange("p (b m x) -> p m b x", b=B, x=P)[:, 2 * mp:2 * mp + 2, :, :]
                            for w in (a_hi, a_lo)]
                    dve.wait_ge(grp_hi, i + 1)
                    nc.vector.tensor_tensor(view[1], bank.rearrange("p (m b x) -> p m b x", m=2, b=B),
                                            as_f32(view[0]), ALU.subtract).then_inc(grp_dve, 1)
                if kind == "VW":
                    dve.wait_ge(grp_hi, 8 + i + 1)
                    nc.vector.scalar_tensor_tensor(vw[:, 2 * i:2 * i + 2, D:2 * D],
                                                   bank.rearrange("p (m n) -> p m n", m=2), tg[:, 0:1],
                                                   as_f32(vw[:, 2 * i:2 * i + 2, 0:D]), ALU.mult,
                                                   ALU.subtract).then_inc(grp_dve, 1)
            for g in groups[:EARLY]:
                group(*g)

            def value_groups():
                dve.wait_ge(tanh_done, 1)
                nc.vector.tensor_scalar(bo_parts[:, 0:D], bo_row[:, :], tg[0:1, 0:1], None, ALU.mult).then_inc(tgbo_ready, 1)
                dve.wait_ge(tgbo_ready, 1)
                nc.vector.scalar_tensor_tensor(bo_parts[:, D:2 * D], bo_row[:, :], tg[0:1, 0:1],
                                               as_f32(bo_parts[:, 0:D]), ALU.mult, ALU.subtract).then_inc(tgbo_ready, 1)
                dve.wait_ge(rows_ready, 1)
                nc.vector.tensor_copy(one_r[:, :], ones_row[:, :]).then_inc(tgbo_ready, 1)
                x_stats(1)
                for g in groups[EARLY:]:
                    group(*g)

            def step(s, par):
                t = s - LAG
                if active(t):
                    tile = xt[:, ds(t, 1), :].rearrange("p o d -> p (o d)")
                    dve.wait_ge(out_done, t + 1)
                    nc.vector.tensor_tensor(tile, ps[:, 6, D:2 * D], tile, ALU.add).then_inc(x1a_done, 1)
                    dve.wait_ge(x1a_done, t + 1)
                    nc.vector.tensor_tensor(tile, ps[:, 6, 0:D], tile, ALU.add).then_inc(x1_done, 1)
                    dve.wait_ge(x1_done, t + 1)
                    nc.vector.bn_stats(stats2[:, ds(t, 1), :].rearrange("p o s -> p (o s)"), tile).then_inc(stats_done, 1)
                t = s - 2
                if active(t):
                    for half in range(2):
                        dve.wait_ge(phi_ready, 2 * t + half + 1)
                        nc.vector.tensor_tensor(pT_lo[:, par, 4 * half:4 * half + 4, :],
                                                ps[:, 4 + half, :].rearrange("p (m i) -> p m i", m=4),
                                                as_f32(pT_hi[:, par, 4 * half:4 * half + 4, :]),
                                                ALU.subtract).then_inc(plo_ready, 1)
                t = s - 1
                if active(t):
                    q = (par - 1) % 2
                    dve.wait_ge(exp_done, t + 1)
                    nc.vector.tensor_reduce(sm[:, q, 0:H // 2], sx[:, q, 0:BANK].rearrange("p (h m) -> p h m", m=M),
                                            AX, ALU.add).then_inc(sum_done, 1)
                    dve.wait_ge(sum_done, t + 1)
                    dve.wait_ge(head_done, t + 1)
                    wait_pos(dve, mul_done, t - 1)
                    nc.vector.reciprocal(rs[:, q, :], sm[:, q, :]).then_inc(recip_done, 1)
                for y in norm_tiles(s):
                    y_low(y, 7, y % 2 * D, norm_tiles(s)[-1] + 1)
                t = s
                if active(t):
                    dve.wait_ge(scores_done, t + 1)
                    sc = ps[:, 2 * par:2 * par + 2, :].rearrange("p a (h m) -> p (a h) m", m=M)
                    nc.vector.tensor_reduce(mx[:, par, :], sc, AX, ALU.max, negate=True).then_inc(max_done, 1)
                t = s + 1
                if active(t):
                    q = (par + 1) % 2
                    dve.wait_ge(xhi_ready, t + 1)
                    nc.vector.tensor_tensor(xT_lo[:, q, :, :], ps[:, 7, 0:D].rearrange("p (k i) -> p k i", k=KD),
                                            as_f32(xT_hi[:, q, :, :]), ALU.subtract).then_inc(xlo_ready, 1)
                t = s
                if active(t):
                    dve.wait_ge(max_done, t + 1)
                    wait_pos(dve, pT_done, 2 * (t - 1))
                    nc.vector.tensor_tensor(sx[:, par, 0:BANK].rearrange("p (h m) -> p h m", m=M),
                                            sc[:, 0:H // 2, :],
                                            mx[:, par, 0:H // 2].unsqueeze(2).broadcast_to([P, H // 2, M]),
                                            ALU.add).then_inc(sub_done, 1)
                if isinstance(s, int):
                    for y in norm_tiles(s + 1):
                        y_tile(y, 2 * (s + 1 - Y_FROM))
            def y_tile(t, done):
                wait_pos(dve, yT_done, done)
                nc.vector.tensor_scalar(yb[:, t % 2, :], xt[:, t, :], mean2[:, t:t + 1], rstd2[:, t:t + 1],
                                        ALU.subtract, ALU.mult).then_inc(y_ready, 1)

            def y_low(t, bank, c0, until):
                dve.wait_ge(yhi_ready, until)
                nc.vector.tensor_tensor(yT_lo[:, :, t * P:(t + 1) * P],
                                        ps[:, bank, c0:c0 + D].rearrange("p (k i) -> p k i", k=KD),
                                        as_f32(yT_hi[:, :, t * P:(t + 1) * P]), ALU.subtract).then_inc(ylo_ready, 1)

            def norm_begins():
                dve.wait_ge(stats_done, NT + TB)
                norm(0, mean2, rstd2)
                for y in norm_tiles(Y_FROM):
                    y_tile(y, 0)

            def route(b):
                link(nc.vector.tensor_reduce(rep[:, :, b:b + 1], ysum[:, :, b * TB:(b + 1) * TB], AX, ALU.add))
                nc.vector.tensor_scalar(rep[:, :, b:b + 1], rep[:, :, b:b + 1], 1.0 / S, None,
                                        ALU.mult).then_inc(rep_ready, 1)
                dve.wait_ge(logits_done, b + 1)
                lg = ps[0:1, LOGITS[b], 0:E]
                link(nc.vector.tensor_reduce(row[:, 10, 0:1], lg, AX, ALU.max))
                nc.vector.tensor_scalar(row[:, 1, :], lg, row[:, 10, 0:1], None, ALU.subtract).then_inc(route_sub, 1)
                dve.wait_ge(route_exp, b + 1)
                link(nc.vector.tensor_reduce(row[:, 11, 0:1], row[:, 2, :], AX, ALU.add))
                link(nc.vector.reciprocal(row[:, 12, 0:1], row[:, 11, 0:1]))
                link(nc.vector.tensor_scalar(row[:, 3, :], row[:, 2, :], row[:, 12, 0:1], None, ALU.mult))
                link(nc.vector.max(row[:, 4, :], row[:, 3, :]))
                nc.vector.max_index(idx[:, b, :], row[:, 4, :], row[:, 3, :]).then_inc(idx_ready, 1)
                link(nc.vector.tensor_tensor(row[:, 7, 0:1], row[:, 4, 0:1], row[:, 4, 1:2], ALU.add))
                dve.wait_ge(idx_ready, b + 1)
                nc.vector.tensor_copy(row[:, 6, :], idx[:, b, :])
                link(nc.vector.reciprocal(row[:, 8, 0:1], row[:, 7, 0:1]))
                link(nc.vector.tensor_scalar(row[:, 9, 0:TOP], row[:, 4, 0:TOP], row[:, 8, 0:1], None, ALU.mult))
                link(nc.vector.tensor_scalar(row[:, 13, 0:TOP], row[:, 9, 0:TOP], tg[0:1, 1:2], None, ALU.mult))
                for slot in range(TOP):
                    last = nc.vector.tensor_scalar(hot[:, slot, :], iota_row[:, :], row[:, 6, slot:slot + 1],
                                                   None, ALU.is_equal)
                link(last)
                link(nc.vector.tensor_scalar(hot[:, TOP, :], hot[:, 0, :], row[:, 13, 0:1], None, ALU.mult))
                nc.vector.scalar_tensor_tensor(hot[:, TOP, :], hot[:, 1, :], row[:, 13, 1:2], hot[:, TOP, :],
                                               ALU.mult, ALU.add).then_inc(hot_ready, 1)

            def route_read(b):
                dve.wait_ge(hotT_done, b + 1)
                nc.vector.tensor_copy(hotT[:, :], ps[0:E, LOGITS[b], 16:16 + TOP + 1]).then_inc(hotT_ready, 1)
                dve.wait_ge(sel_done, b + 1)
                sel = ps[:, LOGITS[b] + 1, :]
                nc.vector.tensor_copy(b1sel[:, b, :, :], sel[:, 0:NF * TOP].rearrange("p (f q) -> p f q", q=TOP))
                nc.vector.tensor_copy(b2sel[:, b, :], sel[:, 32:32 + KD])
                link(nc.vector.tensor_copy(swt[:, b * TOP:(b + 1) * TOP], sel[:, 64:64 + TOP]))
                dve.sem_inc(sel_ready, 1)

            run_steps(dve, step, value_groups, norm_begins, lambda: route(0))
            route_read(0)

            dve.wait_ge(stats_done, 2 * NT)
            norm(1, mean2, rstd2)
            y_tile(TB, TB)
            y_tile(TB + 1, TB)
            dve.wait_ge(w_hi_done, 1)
            nc.vector.tensor_tensor(w1_lo[0][:, :, :], stage_w1[0][:, :, :], as_f32(w1_hi[0][:, :, :]),
                                    ALU.subtract).then_inc(w_lo_done, 1)
            dve.wait_ge(w_hi_done, 2)
            nc.vector.scalar_tensor_tensor(w2_lo[0][:, :, :], stage_w2[0][:, :, :], swt[:, 0:1],
                                           as_f32(w2_hi[0][:, :, :]), ALU.mult, ALU.subtract).then_inc(w_lo_done, 1)

            for t in range(TB, NT):
                if t + 2 < NT:
                    y_tile(t + 2, t + 1)
                y_low(t, 6 + t % 2, 0, t + 1)
            route(1)

            def second_residual(pair):
                tiles = xt[:, 2 * pair:2 * pair + 2, :]
                dve.wait_ge(oTT_done, pair + 1)
                nc.vector.tensor_tensor(tiles, ps[:, 6 + pair % 2, :].rearrange("p (t d) -> p t d", t=2), tiles,
                                        ALU.add).then_inc(x2_done, 1)

            dve.sem_inc(hlo_ready, FREE_GELS)
            for q in range(NQ):
                b, slot = q // TOP, q % TOP
                with dve.Fori(0, NCH) as c:
                    for f in range(NF):
                        n = (c + q * NCH) * NF + f
                        dve.wait_ge(gelu_done, n + 1 + FREE_BANKS)
                        dve.wait_ge(w2_done, n + 1)
                        nc.vector.tensor_copy(h_hi[:, f % 4, :], gel[:, f % 2, :]).then_inc(hhi_ready, 1)
                        dve.wait_ge(hhi_ready, n + 1)
                        nc.vector.tensor_tensor(h_lo[:, f % 4, :], gel[:, f % 2, :], as_f32(h_hi[:, f % 4, :]),
                                                ALU.subtract).then_inc(hlo_ready, 1)
                        if q + 1 < NQ:
                            nxt = 1 - slot
                            dve.wait_ge(w_hi_done, n * 2 + 3)
                            nc.vector.tensor_tensor(w1_lo[nxt][:, ds(c, 1), f * P:(f + 1) * P],
                                                    stage_w1[nxt][:, ds(c, 1), f * P:(f + 1) * P],
                                                    as_f32(w1_hi[nxt][:, ds(c, 1), f * P:(f + 1) * P]),
                                                    ALU.subtract).then_inc(w_lo_done, 1)
                            dve.wait_ge(w_hi_done, n * 2 + 4)
                            nc.vector.scalar_tensor_tensor(w2_lo[nxt][:, f, ds(c * P, P)],
                                                           stage_w2[nxt][:, f, ds(c * P, P)], swt[:, q + 1:q + 2],
                                                           as_f32(w2_hi[nxt][:, f, ds(c * P, P)]), ALU.mult,
                                                           ALU.subtract).then_inc(w_lo_done, 1)
                if q == 0:
                    route_read(1)
                if q == TOP:
                    second_residual(0)
                    second_residual(1)
            for pair in range(2, NT // 2):
                second_residual(pair)

        @block.tensor
        def _(pe):
            mm = nc.tensor.matmul
            pe.wait_ge(ident_ready, 1)

            def three(acc, hi_w, lo_w, hi_x, lo_x, start, stop):
                mm(acc, hi_w, hi_x, start=start, stop=False)
                mm(acc, hi_w, lo_x, start=False, stop=False)
                return mm(acc, lo_w, hi_x, start=False, stop=stop)

            def group(kind, i):
                n = number[(kind, i)]
                bank = ps[:, GRP_BANK[(kind, i)], :]
                if GRP_BEFORE[(kind, i)]:
                    wait_group_read(pe, *GRP_BEFORE[(kind, i)])
                if kind == "ctxT":
                    pe.wait_ge(ld_ctx, 16)
                    for k in range(KD):
                        last = nc.tensor.transpose(bank[:, k * P:(k + 1) * P], ctx_sb[:, k * P:(k + 1) * P], ident[:, :])
                if kind in ("kT", "vT"):
                    w_sb = wk_sb if kind == "kT" else wv_sb
                    pe.wait_ge(ld_wk if kind == "kT" else ld_wv, 16)
                    wait_group_read(pe, "ctxT", 0)
                    for m in range(4):
                        for k in range(KD):
                            c0 = (4 * i + m) * P
                            last = mm(bank[:, m * P:(m + 1) * P], w_sb[:, k, c0:c0 + P], ctxT[:, k, :],
                                      start=(k == 0), stop=(k == KD - 1))
                if kind == "wqT":
                    pe.wait_ge(ld_wq, 16)
                    for m in range(2):
                        for k in range(KD):
                            c0 = (2 * i + m) * P
                            last = nc.tensor.transpose(bank[:, (m * KD + k) * P:(m * KD + k + 1) * P],
                                                       wq_sb[:, k, c0:c0 + P], ident[:, :])
                if kind == "A":
                    ct, mp = i // 4, i % 4
                    wait_group_read(pe, "kT", mp // 2)
                    wait_group_read(pe, "wqT", mp)
                    for m in range(2):
                        last = mm(bank[:, m * B * P:(m + 1) * B * P], wqT[:, 2 * mp + m, ct * P:(ct + 1) * P],
                                  kbd[:, 2 * mp + m, :, :].rearrange("p b x -> p (b x)"), start=True, stop=True)
                if kind == "VW":
                    b, mp = i // 4, i % 4
                    pe.wait_ge(ld_wo, 16)
                    wait_group_read(pe, "vT", mp // 2)
                    for m in range(2):
                        last = mm(bank[:, m * D:(m + 1) * D], vbd[:, 2 * mp + m, b, :], wo_sb[:, 2 * mp + m, :],
                                  start=True, stop=True)
                last.then_inc(grp_done, 1)
            for g in groups[:EARLY]:
                group(*g)
            wait_group_read(pe, "A", 7)

            def value_groups():
                for g in groups[EARLY:]:
                    group(*g)

            def step(s, par):
                t = s - 2
                if active(t):
                    pe.wait_ge(mul_done, t + 1)
                    for half in range(2):
                        wait_pos(pe, plo_ready, 2 * t + half - 1)
                        for m in range(4):
                            c0 = (4 * half + m) * P
                            last = nc.tensor.transpose(ps[:, 4 + half, m * P:(m + 1) * P],
                                                       sx[:, par, c0:c0 + P], ident[:, :])
                        last.then_inc(pT_done, 1)
                for y in norm_tiles(s):
                    pe.wait_ge(xlo_ready, min(s + 1, NT))
                    y_transpose(y, 7, y % 2 * D)
                t = s
                if active(t):
                    pe.wait_ge(xlo_ready, t + 1)
                    wait_pos(pe, sub_done, t - 1)
                    wait_pos(pe, head_done, t - 1)
                    boff = (t // TB) * HM
                    for c in range(2):
                        for k in range(KD):
                            lo, hi = xT_lo[:, par, k, :], xT_hi[:, par, k, :]
                            wh, wl = (w[:, k, ds(boff + c * BANK, BANK)] for w in (a_hi, a_lo))
                            last = three(ps[:, 2 * par + c, :], hi, lo, wh, wl, k == 0, k == KD - 1)
                    last.then_inc(scores_done, 1)
                t = s + 1
                if active(t):
                    q = (par + 1) % 2
                    pe.wait_ge(xn_ready, t + 1)
                    wait_pos(pe, xlo_ready, t)
                    if len(norm_tiles(s)):
                        pe.wait_ge(ylo_ready, norm_tiles(s)[-1] + 1)
                    for k in range(KD):
                        last = nc.tensor.transpose(ps[:, 7, k * P:(k + 1) * P], xn[:, q, k * P:(k + 1) * P], ident[:, :])
                    last.then_inc(xT_done, 1)
                t = s - 2
                if active(t):
                    wait_pos(pe, x1_done, t)
                    bm = (t // TB) * NP
                    if isinstance(t, int) and t == 0:
                        pe.wait_ge(tgbo_ready, 3)
                    mm(ps[:, 6, :], one_r[:, :], bo_parts[:, :], start=True, stop=False)
                    for m in range(NP):
                        if m % 4 == 0:
                            pe.wait_ge(plo_ready, 2 * t + m // 4 + 1)
                        mm(ps[:, 6, :], pT_hi[:, par, m, :], vw[:, ds(bm + m, 1), :].rearrange("p o n -> p (o n)"),
                           start=False, stop=False)
                        last = mm(ps[:, 6, 0:D], pT_lo[:, par, m, :],
                                  vw[:, ds(bm + m, 1), 0:D].rearrange("p o n -> p (o n)"),
                                  start=False, stop=(m == NP - 1))
                    last.then_inc(out_done, 1)
            def y_transpose(t, bank, c0):
                pe.wait_ge(y_ready, t + 1)
                for k in range(KD):
                    last = nc.tensor.transpose(ps[:, bank, c0 + k * P:c0 + (k + 1) * P],
                                               yb[:, t % 2, k * P:(k + 1) * P], ident[:, :])
                last.then_inc(yT_done, 1)

            def route(b):
                pe.wait_ge(rep_ready, b + 1)
                for k in range(KD):
                    last = mm(ps[0:1, LOGITS[b], 0:E], rep[:, k, b:b + 1], gate_sb[:, k, :],
                              start=(k == 0), stop=(k == KD - 1))
                last.then_inc(logits_done, 1)

            def route_select(b):
                pe.wait_ge(hot_ready, b + 1)
                for r in range(TOP + 1):
                    last = mm(ps[0:E, LOGITS[b], 16 + r:17 + r], hot[:, r, :], ones_row[0:1, 0:1],
                              start=True, stop=True)
                last.then_inc(hotT_done, 1)
                pe.wait_ge(hotT_ready, b + 1)
                pe.wait_ge(ld_b12, 32)
                sel = ps[:, LOGITS[b] + 1, :]
                for f in range(NF):
                    mm(sel[:, f * TOP:(f + 1) * TOP], b1_sb[:, f * P:(f + 1) * P], hotT[:, 0:TOP], start=True, stop=True)
                for k in range(KD):
                    mm(sel[:, 32 + k:33 + k], b2_sb[:, k * P:(k + 1) * P], hotT[:, TOP:TOP + 1], start=True, stop=True)
                mm(sel[:, 64:64 + TOP], ones_row[:, :], row[:, 13, 0:TOP], start=True, stop=True).then_inc(sel_done, 1)

            def route_first():
                pe.wait_ge(sub_done, NT - 1)
                pe.wait_ge(head_done, NT - 1)
                pe.wait_ge(ylo_ready, TB)
                route(0)

            run_steps(pe, step, value_groups, route=route_first)
            route_select(0)

            pe.wait_ge(x1_done, NT)
            pe.wait_ge(xlo_ready, NT)
            pe.wait_ge(ylo_ready, TB)
            for t in range(TB, NT):
                if t >= TB + 2:
                    pe.wait_ge(ylo_ready, t - 1)
                y_transpose(t, 6 + t % 2, 0)
            pe.wait_ge(ylo_ready, NT)
            route(1)
            pe.wait_ge(sub_done, NT)
            pe.wait_ge(head_done, NT)
            pe.wait_ge(sel_ready, 1)
            pe.sem_inc(w2_done, FREE_SPLITS)

            def first_layer(q, c, f):
                slot, n = q % TOP, (c + q * NCH) * NF + f
                tok = (c + q // TOP * NCH) * CH
                pe.wait_ge(gelu_done, n + 1)
                for k in range(KD):
                    hi, lo = (w[slot][:, k, f * P:(f + 1) * P] for w in (w1_hi, w1_lo))
                    last = three(ps[:, 4 + f % 2, :], hi, lo, yT_hi[:, k, ds(tok, CH)], yT_lo[:, k, ds(tok, CH)],
                                 k == 0, k == KD - 1)
                last.then_inc(h_done, 1)

            def second_layer(q, c, f):
                slot, n = q % TOP, (c + q * NCH) * NF + f
                if f == 0 and q >= TOP:
                    pe.wait_ge(oT_ready, q // TOP * NCH * KD)
                pe.wait_ge(hlo_ready, n + 1 + FREE_GELS)
                for d in range(KD):
                    hi, lo = (w[slot][:, f, d * P:(d + 1) * P] for w in (w2_hi, w2_lo))
                    acc = ps[:, ds(c * KD + d, 1), :].rearrange("p o n -> p (o n)")
                    last = three(acc, hi, lo, h_hi[:, f % 4, :], h_lo[:, f % 4, :],
                                 slot == 0 and f == 0, slot == TOP - 1 and f == NF - 1)
                last.then_inc(w2_done, 1)

            def back(pair):
                c = pair // (CH // P // 2)
                pe.wait_ge(oT_ready, (c + 1) * KD)
                if pair >= 2:
                    pe.wait_ge(x2_done, pair - 1)
                for j in range(2 * KD):
                    t0 = (2 * pair + j // KD) * P % S
                    last = nc.tensor.transpose(ps[:, 6 + pair % 2, j * P:(j + 1) * P],
                                               oT[:, j % KD, t0:t0 + P], ident[:, :])
                last.then_inc(oTT_done, 1)

            for q in range(NQ):
                b, slot = q // TOP, q % TOP
                with pe.Fori(0, NCH) as c:
                    pe.wait_ge(w_lo_done, q * (2 * NCH * NF) + 2)
                    for f in range(NF):
                        first_layer(q, c, f)
                        if f >= 2:
                            second_layer(q, c, f - 2)
                    second_layer(q, c, NF - 2)
                    second_layer(q, c, NF - 1)
                if q == 0:
                    route_select(1)
                if q == TOP:
                    back(0)
                    back(1)
            for pair in range(2, NT // 2):
                back(pair)

_INS = ["x", "ctx_1024", "g_xattn", "g_ffn", "L0_xattn_Wq", "L0_xattn_Wk", "L0_xattn_Wv", "L0_xattn_Wo",
        "L0_xattn_bo", "L0_ffn_gate_w", "L0_ffn_w1", "L0_ffn_b1", "L0_ffn_w2", "L0_ffn_b2"]


def kernel(**inputs):
    import numpy as _np
    import concourse.bacc as _bacc
    from concourse import mybir as _mybir
    from concourse.bass_utils import run_bass_kernel_spmd as _run

    nc = _bacc.Bacc("TRN2", target_bir_lowering=False, num_devices=1)
    arrays, args = {}, []
    for name in _INS:
        a = _np.ascontiguousarray(inputs[name])
        arrays[f"in_{name}_dram"] = a
        args.append(nc.dram_tensor(f"in_{name}_dram", a.shape, _mybir.dt.from_np(a.dtype), kind="ExternalInput").ap())
    shape = inputs["x"].shape
    out = nc.dram_tensor("out_0_dram", (shape[0] * shape[1], shape[2]), _mybir.dt.float32,
                         kind="ExternalOutput").ap()
    gated_cross_attention_moe_kernel(nc, *args, out)
    r = _run(nc, [arrays], core_ids=[0])
    return r.results[0]["out_0_dram"].reshape(shape)
```

```python
import concourse.bass as bass
from concourse import mybir
from contextlib import ExitStack


def gated_cross_attention_moe_kernel(nc, x, ctx_tokens, g_xattn, g_ffn, Wq, Wk, Wv, Wo, bo,
                                     gate_w, w1, b1, w2, b2, out):
    f32 = mybir.dt.float32
    f32r = mybir.dt.float32r
    u32 = mybir.dt.uint32
    i32 = mybir.dt.int32
    ALU = mybir.AluOpType
    ACT = mybir.ActivationFunctionType
    AX = mybir.AxisListType.X
    ds = bass.ds

    P = 128
    B, S, D = x.shape
    M = ctx_tokens.shape[1]
    HD = Wq.shape[1]
    DH = 64
    H = HD // DH
    E, _, F = w1.shape
    TOP = 2
    NT = B * S // P
    TB = S // P
    KD = D // P
    NP = HD // P
    NF = F // P
    HM = H * M
    CH = 512
    NCH = S // CH
    BANK = 512
    NQ = B * TOP
    SCALE = DH ** -0.5
    EPS = 1e-5
    LEAD, LAG = 2, 3
    assert 2 * DH == P and 2 * M == P and B * M == P and TOP == 2 and NCH == 2 and KD == 2

    xf = x.rearrange("b s d -> (b s) d")

    cursor = [(nc.sbuf_base + 63) // 64 * 64]

    def place(name, shape, dtype=f32, at=None):
        size = 4
        for n in shape[1:]:
            size *= n
        offset = cursor[0] if at is None else at[0]
        t = nc.alloc_sbuf_tensor_at(name, shape, dtype, offset=offset)
        (cursor if at is None else at)[0] = offset + (size + 31) // 32 * 32
        return t

    xt = place("xt", [P, NT, D])
    yT_hi = place("yT_hi", [P, KD, NT * P], f32r)
    yT_lo = place("yT_lo", [P, KD, NT * P], f32r)
    ident = place("ident", [P, P])
    gate_sb = place("gate_sb", [P, KD, E])
    stats1 = place("stats1", [P, NT, 6])
    stats2 = stats1
    mean1 = place("mean1", [P, NT])
    rstd1 = place("rstd1", [P, NT])
    mean2 = place("mean2", [P, NT])
    rstd2 = place("rstd2", [P, NT])
    ve = place("ve", [P, TB])
    dm = place("dm", [P, TB])
    nu = place("nu", [P, TB])
    half_bits = place("half_bits", [P, TB], i32)
    gg = place("gg", [P, 2])
    tg = place("tg", [P, 2])
    mx = place("mx", [P, 2, H])
    sm = place("sm", [P, 2, H])
    rs = place("rs", [P, 2, H])
    ysum = place("ysum", [P, KD, NT])
    rep = place("rep", [P, KD, B])
    row = place("row", [1, 16, E])
    idx = place("idx", [1, B, E], u32)
    hot = place("hot", [1, TOP + 1, E])
    hotT = place("hotT", [E, TOP + 1])
    ones_row = place("ones_row", [1, P])
    iota_row = place("iota_row", [1, E])
    b1sel = place("b1sel", [P, B, NF, TOP])
    b2sel = place("b2sel", [P, B, KD])
    swt = place("swt", [P, NQ])
    bo_row = place("bo_row", [1, D])
    bo_parts = place("bo_parts", [1, 2 * D], f32r)
    one_r = place("one_r", [1, P], f32r)
    warm = place("warm", [1, 2])

    first = [cursor[0]]
    wq_sb = place("wq_sb", [P, KD, HD], at=first)
    wk_sb = place("wk_sb", [P, KD, HD], at=first)
    wv_sb = place("wv_sb", [P, KD, HD], at=first)
    wo_sb = place("wo_sb", [P, NP, D], at=first)
    wqT = place("wqT", [P, NP, D], at=first)
    kbd = place("kbd", [P, NP, B, P], at=first)
    vbd = place("vbd", [P, NP, B, P], at=first)
    ctx_sb = place("ctx_sb", [P, D], at=first)
    ctxT = place("ctxT", [P, KD, P], at=first)
    first2 = [cursor[0]]
    stage_w1 = [place("stage_w1_0", [P, KD, F], at=first2)]
    stage_w2 = [place("stage_w2_0", [P, NF, D], at=first2)]
    w1_hi = [place("w1_hi_0", [P, KD, F], f32r, at=first2)]
    w1_lo = [place("w1_lo_0", [P, KD, F], f32r, at=first2)]
    w2_hi = [place("w2_hi_0", [P, NF, D], f32r, at=first2)]
    w2_lo = [place("w2_lo_0", [P, NF, D], f32r, at=first2)]
    first3 = [first2[0]]
    oT = place("oT", [P, KD, S], at=first2)
    b1_sb = place("b1_sb", [E, F], at=first3)
    b2_sb = place("b2_sb", [E, D], at=first3)
    yb = place("yb", [P, 2, D], at=first3)
    assert first3[0] <= first2[0]

    second = [max(first[0], first2[0])]
    second2 = [second[0]]
    a_hi = place("a_hi", [P, KD, B * HM], f32r, at=second)
    a_lo = place("a_lo", [P, KD, B * HM], f32r, at=second)
    vw = place("vw", [P, B * NP, 2 * D], f32r, at=second)
    sx = place("sx", [P, 2, HM], at=second)
    third = [second[0]]
    pT_hi = place("pT_hi", [P, 2, NP, P], f32r, at=second)
    pT_lo = place("pT_lo", [P, 2, NP, P], f32r, at=second)
    xT_hi = place("xT_hi", [P, 2, KD, P], f32r, at=second)
    xT_lo = place("xT_lo", [P, 2, KD, P], f32r, at=second)
    xn = place("xn", [P, 2, D], at=second)
    stage_w1.append(place("stage_w1_1", [P, KD, F], at=second2))
    stage_w2.append(place("stage_w2_1", [P, NF, D], at=second2))
    w1_hi.append(place("w1_hi_1", [P, KD, F], f32r, at=second2))
    w1_lo.append(place("w1_lo_1", [P, KD, F], f32r, at=second2))
    w2_hi.append(place("w2_hi_1", [P, NF, D], f32r, at=second2))
    w2_lo.append(place("w2_lo_1", [P, NF, D], f32r, at=second2))
    gel = place("gel", [P, 2, CH], at=second2)
    h_hi = place("h_hi", [P, 4, CH], f32r, at=second2)
    h_lo = place("h_lo", [P, 4, CH], f32r, at=third)
    assert second2[0] <= third[0] and third[0] <= second[0]

    def as_f32(ap):
        return ap.bitcast(f32)

    stack = ExitStack()
    with stack:
        ps = stack.enter_context(nc.psum_tensor("ps", [P, 8, BANK], f32))

        def sem(name):
            return stack.enter_context(nc.semaphore(name))

        ld_ctx, ld_wk, ld_wq, ld_wv, ld_wo = (sem("ld_" + n) for n in ("ctx", "wk", "wq", "wv", "wo"))
        ld_x = [sem(f"ld_x_{b}") for b in range(B)]
        ld_small, ld_b12 = sem("ld_small"), sem("ld_b12")
        ident_ready, zeros_ready, rows_ready = sem("ident_ready"), sem("zeros_ready"), sem("rows_ready")
        tanh_done, tgbo_ready = sem("tanh_done"), sem("tgbo_ready")
        grp_done, grp_act, grp_dve = sem("grp_done"), sem("grp_act"), sem("grp_dve")
        grp_hi = sem("grp_hi")
        stats_done, ln_step = sem("stats_done"), sem("ln_step")
        ln_ready, xc_ready = sem("ln_ready"), sem("xc_ready")
        xn_ready, xT_done, xhi_ready, xlo_ready = (
            sem(n) for n in ("xn_ready", "xT_done", "xhi_ready", "xlo_ready"))
        scores_done, head_done, max_done, sub_done, exp_done, sum_done, recip_done, mul_done = (
            sem(n) for n in ("scores_done", "head_done", "max_done", "sub_done", "exp_done", "sum_done",
                             "recip_done", "mul_done"))
        pT_done, phi_ready, plo_ready, out_done, x1a_done, x1_done = (
            sem(n) for n in ("pT_done", "phi_ready", "plo_ready", "out_done", "x1a_done", "x1_done"))
        y_ready, yT_done, yhi_ready, ylo_ready = (
            sem(n) for n in ("y_ready", "yT_done", "yhi_ready", "ylo_ready"))
        rep_ready, logits_done, route_step, route_sub, route_exp, idx_ready, hot_ready, hotT_done, hotT_ready, sel_done, sel_ready = (
            sem(n) for n in ("rep_ready", "logits_done", "route_step", "route_sub", "route_exp", "idx_ready", "hot_ready",
                             "hotT_done", "hotT_ready", "sel_done", "sel_ready"))
        staged_w1 = [sem("staged_w1_0"), sem("staged_w1_1")]
        staged_w2 = [sem("staged_w2_0"), sem("staged_w2_1")]
        w_hi_done, w_lo_done = sem("w_hi_done"), sem("w_lo_done")
        h_done, gelu_done, hhi_ready, hlo_ready, w2_done = (
            sem(n) for n in ("h_done", "gelu_done", "hhi_ready", "hlo_ready", "w2_done"))
        FREE_BANKS, FREE_GELS, FREE_SPLITS = 2, 2, 4
        PIECES0 = 4
        Y1_FROM = 5
        MEANS_AT, LOGITS_AT, PROBS_AT, SHARES_AT, SELECT_AT = 8, 10, 11, 12, 14

        PIECES = [0, 0, 0, 0, 2, 1, 1, 1, 1, 2, 2, 1, 2, 1, 2, 0]
        assert sum(PIECES) == len(PIECES) == NCH * NF

        def y1_tiles(n):
            return range(TB + 2 * (n - Y1_FROM), TB + 2 * (n - Y1_FROM) + 2) if Y1_FROM <= n < Y1_FROM + TB // 2 else ()

        def pieces(q, c, f):
            if q + 1 == NQ:
                return []
            if q > 0:
                return [(c, f)]
            n = c * NF + f
            return [(i // NF, i % NF) for i in range(sum(PIECES[:n]), sum(PIECES[:n + 1]))]

        FINISH_AT = (1, 1)

        def back_pair(c, f):
            return {(0, 1): 0, (0, 2): 1, (0, 3): 2, (0, 4): 3, (1, 3): 4, (1, 4): 5}.get((c, f))

        def sum_is_through(eng, b, c):
            eng.wait_ge(w2_done, ((b * TOP + TOP - 1) * NCH + c + 1) * NF + FREE_SPLITS)
            if b > 0:
                eng.wait_ge(oTT_done, (b - 1) * (TB // 2) + (c + 1) * (TB // 2 // NCH))

        def over_chunks(eng, q, body):
            if q in (0, NQ - 1):
                for c in range(NCH):
                    body(c)
            else:
                with eng.Fori(0, NCH) as c:
                    body(c)
        oT0_ready, oT1_ready, oTT_done, x2_done, stored = (
            sem(n) for n in ("oT0_ready", "oT1_ready", "oTT_done", "x2_done", "stored"))

        groups = ([("ctxT", 0)] + [("kT", i) for i in range(2)] + [("wqT", i) for i in range(4)]
                  + [("A", i) for i in range(8)] + [("vT", i) for i in range(2)]
                  + [("VW", i) for i in range(8)])
        number = {g: n for n, g in enumerate(groups)}
        EARLY = number[("vT", 0)]
        GRP_BANK = {g: n % 8 if n < EARLY else 4 + (n - EARLY) % 3 for n, g in enumerate(groups)}
        GRP_BEFORE = {g: next((h for h in reversed(groups[:n]) if GRP_BANK[h] == GRP_BANK[g]), None)
                      for n, g in enumerate(groups)}
        reader = {}
        counts = {"act": 0, "dve": 0}
        for kind, i in groups:
            who = "act" if kind in ("kT", "wqT", "vT") and i % 2 == 0 else "dve"
            counts[who] += 1
            reader[(kind, i)] = (who, counts[who])

        def wait_group_read(eng, kind, i):
            who, n = reader[(kind, i)]
            eng.wait_ge(grp_act if who == "act" else grp_dve, n)

        LOGITS = [0, 6]
        STEPS = list(range(-LEAD, NT + LAG))
        Y_FROM = TB + LAG + 1
        ROUTE_AT = Y_FROM + TB // 2
        LOOP0, LOOP1 = LAG + 1, Y_FROM
        assert (LOOP1 - LOOP0) % 2 == 0 and ROUTE_AT == NT

        def run_steps(eng, step, value_groups=lambda: None, norm_begins=lambda: None, route=lambda: None,
                      before_last=lambda s: None):
            for s in STEPS:
                if s == 1:
                    value_groups()
                if s < LOOP0:
                    step(s, s % 2)
            with eng.Fori(0, (LOOP1 - LOOP0) // 2) as i:
                step(LOOP0 + i * 2, 0)
                step(LOOP0 + 1 + i * 2, 1)
            for s in STEPS:
                if s >= LOOP1:
                    if s == Y_FROM:
                        norm_begins()
                    if s == ROUTE_AT:
                        route()
                    if s > ROUTE_AT:
                        before_last(s)
                    step(s, s % 2)

        def norm_tiles(s):
            return range(2 * (s - Y_FROM), 2 * (s - Y_FROM) + 2) if isinstance(s, int) and Y_FROM <= s < ROUTE_AT else ()

        def active(t):
            return not isinstance(t, int) or 0 <= t < NT

        def wait_pos(eng, s, v):
            if not isinstance(v, int) or v > 0:
                eng.wait_ge(s, v)

        block = stack.enter_context(nc.Block())

        @block.sync
        def _(sp):
            def load_x(b):
                sp.dma_start(xt[:, b * TB:(b + 1) * TB, :],
                             xf[b * S:(b + 1) * S, :].rearrange("(t p) d -> p t d", p=P)).then_inc(ld_x[b], 16)

            sp.dma_start(ctx_sb[:, :], ctx_tokens.rearrange("b m d -> (b m) d")).then_inc(ld_ctx, 16)
            sp.dma_start(wk_sb[:, :, :], Wk.rearrange("(k p) n -> p k n", p=P)).then_inc(ld_wk, 16)
            sp.dma_start(wq_sb[:, :, :], Wq.rearrange("(k p) n -> p k n", p=P)).then_inc(ld_wq, 16)
            load_x(0)
            sp.dma_start(wv_sb[:, :, :], Wv.rearrange("(k p) n -> p k n", p=P)).then_inc(ld_wv, 16)
            sp.dma_start(wo_sb[:, :, :], Wo.rearrange("(k p) n -> p k n", p=P)).then_inc(ld_wo, 16)
            load_x(1)

            sp.wait_ge(grp_done, len(groups))
            sp.dma_start(b1_sb[:, :], b1).then_inc(ld_b12, 16)
            sp.dma_start(b2_sb[:, :], b2).then_inc(ld_b12, 16)

            for q in range(NQ):
                b, slot = q // TOP, q % TOP
                if q < TOP:
                    sp.wait_ge(*((x1_done, 1) if slot == 0 else (out_done, NT)))
                else:
                    sp.wait_ge(w_lo_done, PIECES0 + 2 * NCH * NF * (q - TOP))
                sp.wait_ge(idx_ready, b + 1)
                e = sp.value_load(idx[0:1, b, slot:slot + 1], min_val=0, max_val=E - 1)
                sp.dma_start(stage_w1[slot][:, :, :],
                             w1[ds(e, 1), :, :].rearrange("o (k p) n -> p (o k) n", p=P)).then_inc(staged_w1[slot], 16)
                sp.dma_start(stage_w2[slot][:, :, :],
                             w2[ds(e, 1), :, :].rearrange("o (k p) n -> p (o k) n", p=P)).then_inc(staged_w2[slot], 16)

            with sp.Fori(0, NT // 2) as i:
                sp.wait_ge(x2_done, i + 1)
                sp.dma_start(out[ds(i * 2 * P, 2 * P), :].rearrange("(t p) d -> p t d", p=P),
                             xt[:, ds(i * 2, 2), :]).then_inc(stored, 16)
            sp.wait_ge(stored, 16 * (NT // 2))

        @block.gpsimd
        def _(pool):
            nc.gpsimd.memset(ident[:, :], 0.0).then_inc(zeros_ready, 1)
            pool.wait_ge(zeros_ready, 1)
            nc.gpsimd.affine_select(out=ident[:, :], in_=ident[:, :], compare_op=ALU.not_equal, fill=1.0,
                                    base=0, pattern=[[-1, P]], channel_multiplier=1).then_inc(ident_ready, 1)
            nc.gpsimd.memset(kbd[:, :, :, :], 0.0).then_inc(zeros_ready, 1)
            nc.gpsimd.memset(vbd[:, :, :, :], 0.0).then_inc(zeros_ready, 1)
            nc.gpsimd.memset(ones_row[:, :], 1.0)
            for e in range(E):
                last = nc.gpsimd.memset(iota_row[:, e:e + 1], float(e))
            last.then_inc(rows_ready, 1)

            def step(s, par):
                t = s - 1
                if active(t):
                    q = (par - 1) % 2
                    pool.wait_ge(recip_done, t + 1)
                    pr = sx[:, q, :].rearrange("p (h m) -> p h m", m=M)
                    nc.gpsimd.tensor_tensor(pr, pr, rs[:, q, :].unsqueeze(2).broadcast_to([P, H, M]),
                                            ALU.mult).then_inc(mul_done, 1)
                t = s + LEAD
                if active(t):
                    wait_pos(pool, xT_done, t - 1)
                    tile = xt[:, ds(t, 1), :].rearrange("p o d -> p (o d)")
                    nc.gpsimd.tensor_tensor(xn[:, par, :], tile, mean1[:, ds(t, 1)].broadcast_to([P, D]),
                                            ALU.subtract).then_inc(xc_ready, 1)
                    pool.wait_ge(xc_ready, t + 1)
                    nc.gpsimd.tensor_tensor(xn[:, par, :], xn[:, par, :], rstd1[:, ds(t, 1)].broadcast_to([P, D]),
                                            ALU.mult).then_inc(xn_ready, 1)
            pool.wait_ge(ln_ready, 1)
            run_steps(pool, step)

            pool.wait_ge(ln_ready, 3)
            for t in range(TB, NT):
                pool.wait_ge(yT_done, t - 1)
                nc.gpsimd.tensor_tensor(yb[:, t % 2, :], xt[:, t, :], mean2[:, t:t + 1].broadcast_to([P, D]),
                                        ALU.subtract).then_inc(xc_ready, 1)
                pool.wait_ge(xc_ready, NT + t - TB + 1)
                nc.gpsimd.tensor_tensor(yb[:, t % 2, :], yb[:, t % 2, :], rstd2[:, t:t + 1].broadcast_to([P, D]),
                                        ALU.mult).then_inc(y_ready, 1)

        @block.scalar
        def _(act):
            act.dma_start(gg[:, 0:1], g_xattn.rearrange("(o n) -> o n", o=1).broadcast_to([P, 1])).then_inc(ld_small, 16)
            act.dma_start(gg[:, 1:2], g_ffn.rearrange("(o n) -> o n", o=1).broadcast_to([P, 1])).then_inc(ld_small, 16)
            act.dma_start(bo_row[:, :], bo.rearrange("(o n) -> o n", o=1)).then_inc(ld_small, 16)
            act.dma_start(gate_sb[:, :, :], gate_w.rearrange("(k p) e -> p k e", p=P)).then_inc(ld_small, 16)

            def y_high(t, bank, c0, until):
                act.wait_ge(yT_done, until)
                for k in range(KD):
                    last = nc.scalar.activation(yT_hi[:, k, t * P:(t + 1) * P],
                                                ps[:, bank, c0 + k * P:c0 + (k + 1) * P],
                                                ACT.Copy, accum_out=ysum[:, k, t:t + 1])
                last.then_inc(yhi_ready, 1)

            def route(b):
                act.wait_ge(route_sub, b + 1)
                nc.scalar.activation(row[:, 2, :], row[:, 1, :], ACT.Exp).then_inc(route_exp, 1)

            act.wait_ge(rows_ready, 1)
            nc.scalar.activation(warm[:, 0:1], ones_row[:, 0:1], ACT.Exp)

            def group(kind, i):
                n = number[(kind, i)]
                bank = ps[:, GRP_BANK[(kind, i)], :]
                if kind in ("kT", "vT") and i % 2 == 0:
                    act.wait_ge(grp_done, n + 1)
                    act.wait_ge(zeros_ready, 3)
                    dst = kbd if kind == "kT" else vbd
                    for h in range(2):
                        r = slice(h * DH, (h + 1) * DH)
                        last = nc.scalar.activation(
                            dst[r, 4 * i:4 * i + 4, :, h * M:(h + 1) * M],
                            bank[r, :].rearrange("p (m b j) -> p m b j", m=4, b=B), ACT.Copy,
                            scale=SCALE if kind == "kT" else 1.0)
                    last.then_inc(grp_act, 1)
                if kind == "wqT" and i % 2 == 0:
                    act.wait_ge(grp_done, n + 1)
                    nc.scalar.activation(wqT[:, 2 * i:2 * i + 2, :],
                                         bank.rearrange("p (m c) -> p m c", m=2), ACT.Copy).then_inc(grp_act, 1)
                if kind == "A":
                    act.wait_ge(grp_done, n + 1)
                    ct, mp = i // 4, i % 4
                    dst = a_hi[:, ct, :].rearrange("p (b m x) -> p m b x", b=B, x=P)[:, 2 * mp:2 * mp + 2, :, :]
                    nc.scalar.activation(dst, bank.rearrange("p (m b x) -> p m b x", m=2, b=B),
                                         ACT.Copy).then_inc(grp_hi, 1)
                if kind == "VW":
                    act.wait_ge(grp_done, n + 1)
                    nc.scalar.activation(vw[:, 2 * i:2 * i + 2, 0:D], bank.rearrange("p (m n) -> p m n", m=2),
                                         ACT.Copy, scale=tg[:, 0:1]).then_inc(grp_hi, 1)

            for g in groups[:EARLY]:
                group(*g)
            act.wait_ge(ld_small, 64)
            nc.scalar.activation(tg[:, :], gg[:, :], ACT.Tanh).then_inc(tanh_done, 1)

            def value_groups():
                act.wait_ge(tanh_done, 1)
                for g in groups[EARLY:]:
                    group(*g)

            def step(s, par):
                t = s - 2
                if active(t):
                    for half in range(2):
                        act.wait_ge(pT_done, 2 * t + half + 1)
                        if half == 0:
                            wait_pos(act, out_done, t - 1)
                        nc.scalar.activation(pT_hi[:, par, 4 * half:4 * half + 4, :],
                                             ps[:, 4 + half, :].rearrange("p (m i) -> p m i", m=4),
                                             ACT.Copy).then_inc(phi_ready, 1)
                t = s - 1
                if active(t):
                    q = (par - 1) % 2
                    act.wait_ge(sub_done, t + 1)
                    nc.scalar.activation(sx[:, q, 0:BANK], sx[:, q, 0:BANK], ACT.Exp).then_inc(exp_done, 1)
                for y in norm_tiles(s):
                    y_high(y, 7, y % 2 * D, norm_tiles(s)[-1] + 1)
                t = s + 1
                if active(t):
                    q = (par + 1) % 2
                    act.wait_ge(xT_done, t + 1)
                    wait_pos(act, scores_done, t - 1)
                    nc.scalar.activation(xT_hi[:, q, :, :], ps[:, 7, 0:D].rearrange("p (k i) -> p k i", k=KD),
                                         ACT.Copy).then_inc(xhi_ready, 1)
                t = s
                if active(t):
                    act.wait_ge(max_done, t + 1)
                    wait_pos(act, pT_done, 2 * (t - 1))
                    for h in range(H // 2, H):
                        c0 = h * M
                        last = nc.scalar.activation(sx[:, par, c0:c0 + M], ps[:, 2 * par + 1, c0 - BANK:c0 - BANK + M],
                                                    ACT.Exp, bias=mx[:, par, h:h + 1],
                                                    accum_out=sm[:, par, h:h + 1])
                    last.then_inc(head_done, 1)
            def before_last(s):
                if s == ROUTE_AT + 1:
                    nc.scalar.activation(warm[:, 1:2], ones_row[:, 0:1], ACT.Gelu)

            run_steps(act, step, value_groups, route=lambda: route(0), before_last=before_last)

            act.wait_ge(staged_w1[0], 16)
            for half in range(2):
                cols = slice(half * F // 2, (half + 1) * F // 2)
                nc.scalar.activation(w1_hi[0][:, :, cols], stage_w1[0][:, :, cols], ACT.Copy).then_inc(w_hi_done, 1)
            act.wait_ge(staged_w2[0], 16)
            act.wait_ge(sel_ready, 1)
            for half in range(2):
                rows = slice(half * NF // 2, (half + 1) * NF // 2)
                nc.scalar.activation(w2_hi[0][:, rows, :], stage_w2[0][:, rows, :], ACT.Copy,
                                     scale=swt[:, 0:1]).then_inc(w_hi_done, 1)

            def finish(b, c):
                sum_is_through(act, b, c)
                nc.scalar.activation(oT[:, 0, c * CH:(c + 1) * CH], ps[:, 2 * c, :], ACT.Identity,
                                     bias=b2sel[:, b, 0:1]).then_inc(oT0_ready, 1)

            act.sem_inc(gelu_done, FREE_BANKS)
            for q in range(NQ):
                b, slot = q // TOP, q % TOP
                if slot == 0 and b > 0:
                    for c in range(NCH):
                        finish(b - 1, c)
                if slot == TOP - 1 and b + 1 < B:
                    act.wait_ge(sel_ready, b + 2)
                def chunk(c):
                    for f in range(NF):
                        n = (c + q * NCH) * NF + f
                        act.wait_ge(h_done, n + 1)
                        act.wait_ge(hlo_ready, n + 1)
                        nc.scalar.activation(gel[:, f % 2, :], ps[:, 4 + f % 2, :], ACT.Gelu,
                                             bias=b1sel[:, b, f, slot:slot + 1]).then_inc(gelu_done, 1)
                        if q == 0 and n == PROBS_AT:
                            route(1)
                        for pc, pf in pieces(q, c, f):
                            nxt = 1 - slot
                            if pf == 0:
                                act.wait_ge(w2_done, q * NCH * NF + FREE_SPLITS)
                                act.wait_ge(staged_w1[nxt], ((q + 1) // TOP + 1) * 16)
                                act.wait_ge(staged_w2[nxt], ((q + 1) // TOP + 1) * 16)
                            nc.scalar.activation(w1_hi[nxt][:, ds(pc, 1), pf * P:(pf + 1) * P],
                                                 stage_w1[nxt][:, ds(pc, 1), pf * P:(pf + 1) * P],
                                                 ACT.Copy).then_inc(w_hi_done, 1)
                            nc.scalar.activation(w2_hi[nxt][:, pf, ds(pc * P, P)], stage_w2[nxt][:, pf, ds(pc * P, P)],
                                                 ACT.Copy, scale=swt[:, q + 1:q + 2]).then_inc(w_hi_done, 1)
                        if q == 0:
                            for t in y1_tiles(n):
                                y_high(t, 6 + t % 2, 0, t + 1)
                        if q == NQ - 1 and (c, f) == FINISH_AT:
                            finish(B - 1, 0)
                over_chunks(act, q, chunk)
            finish(B - 1, 1)

        @block.vector
        def _(dve):
            ln = [0]

            def link(ins):
                ln[0] += 1
                ins.then_inc(ln_step, 1)
                dve.wait_ge(ln_step, ln[0])

            def norm(b, mean, rstd, parts=range(4)):
                tiles = slice(b * TB, (b + 1) * TB)
                me, ce, mo, co = (stats1[:, tiles, i] for i in (1, 2, 4, 5))
                m, r = mean[:, tiles], rstd[:, tiles]
                tt, ts, stt = nc.vector.tensor_tensor, nc.vector.tensor_scalar, nc.vector.scalar_tensor_tensor
                if 0 in parts:
                    tt(dm[:, :], me, mo, ALU.subtract)
                    tt(m, me, mo, ALU.add)
                    link(tt(ve[:, :], ce, co, ALU.add))
                    ts(m, m, 0.5, None, ALU.mult)
                    tt(dm[:, :], dm[:, :], dm[:, :], ALU.mult)
                    link(ts(ve[:, :], ve[:, :], 1.0 / D, EPS, ALU.mult, ALU.add))
                    link(stt(ve[:, :], dm[:, :], 0.25, ve[:, :], ALU.mult, ALU.add))
                    link(ts(half_bits[:, :], ve[:, :].bitcast(i32), 1, None, ALU.arith_shift_right))
                    link(ts(r.bitcast(i32), half_bits[:, :], -1.0, float(0x5F3759DF), ALU.mult, ALU.add))
                for part in (1, 2, 3):
                    if part in parts:
                        link(stt(nu[:, :], ve[:, :], -0.5, r, ALU.mult, ALU.mult))
                        link(tt(nu[:, :], nu[:, :], r, ALU.mult))
                        link(stt(r, nu[:, :], 1.5, r, ALU.add, ALU.mult))

            def x_stats(b):
                dve.wait_ge(ld_x[b], 16)
                with dve.Fori(0, TB // 4) as i:
                    for j in range(4):
                        t = i * 4 + (b * TB + j)
                        nc.vector.bn_stats(stats1[:, ds(t, 1), :].rearrange("p o s -> p (o s)"),
                                           xt[:, ds(t, 1), :].rearrange("p o d -> p (o d)")).then_inc(stats_done, 1)

            def x_norm(b, parts=range(4)):
                if 0 in parts:
                    dve.wait_ge(stats_done, (b + 1) * TB)
                norm(b, mean1, rstd1, parts)
                if 3 in parts:
                    dve.sem_inc(ln_ready, 1)

            def group(kind, i):
                n = number[(kind, i)]
                bank = ps[:, GRP_BANK[(kind, i)], :]
                if kind == "ctxT":
                    dve.wait_ge(grp_done, n + 1)
                    nc.vector.tensor_copy(ctxT[:, :, :], bank[:, 0:D].rearrange("p (k i) -> p k i", k=KD)).then_inc(grp_dve, 1)
                if kind in ("kT", "vT") and i % 2 == 1:
                    dve.wait_ge(grp_done, n + 1)
                    dve.wait_ge(zeros_ready, 3)
                    dst = kbd if kind == "kT" else vbd
                    for h in range(2):
                        r = slice(h * DH, (h + 1) * DH)
                        last = nc.vector.tensor_scalar(
                            dst[r, 4 * i:4 * i + 4, :, h * M:(h + 1) * M],
                            bank[r, :].rearrange("p (m b j) -> p m b j", m=4, b=B),
                            SCALE if kind == "kT" else 1.0, None, ALU.mult)
                    last.then_inc(grp_dve, 1)
                if kind == "wqT" and i % 2 == 1:
                    dve.wait_ge(grp_done, n + 1)
                    nc.vector.tensor_copy(wqT[:, 2 * i:2 * i + 2, :],
                                          bank.rearrange("p (m c) -> p m c", m=2)).then_inc(grp_dve, 1)
                if kind == "A" and i == 3:
                    x_stats(0)
                    x_norm(0)
                if kind == "A":
                    ct, mp = i // 4, i % 4
                    view = [w[:, ct, :].rearrange("p (b m x) -> p m b x", b=B, x=P)[:, 2 * mp:2 * mp + 2, :, :]
                            for w in (a_hi, a_lo)]
                    dve.wait_ge(grp_hi, i + 1)
                    nc.vector.tensor_tensor(view[1], bank.rearrange("p (m b x) -> p m b x", m=2, b=B),
                                            as_f32(view[0]), ALU.subtract).then_inc(grp_dve, 1)
                if kind == "VW" and i == 0:
                    x_stats(1)
                if kind == "VW":
                    dve.wait_ge(grp_hi, 8 + i + 1)
                    nc.vector.scalar_tensor_tensor(vw[:, 2 * i:2 * i + 2, D:2 * D],
                                                   bank.rearrange("p (m n) -> p m n", m=2), tg[:, 0:1],
                                                   as_f32(vw[:, 2 * i:2 * i + 2, 0:D]), ALU.mult,
                                                   ALU.subtract).then_inc(grp_dve, 1)
            for g in groups[:EARLY]:
                group(*g)

            def value_groups():
                dve.wait_ge(tanh_done, 1)
                nc.vector.tensor_scalar(bo_parts[:, 0:D], bo_row[:, :], tg[0:1, 0:1], None, ALU.mult).then_inc(tgbo_ready, 1)
                dve.wait_ge(tgbo_ready, 1)
                nc.vector.scalar_tensor_tensor(bo_parts[:, D:2 * D], bo_row[:, :], tg[0:1, 0:1],
                                               as_f32(bo_parts[:, 0:D]), ALU.mult, ALU.subtract).then_inc(tgbo_ready, 1)
                dve.wait_ge(rows_ready, 1)
                nc.vector.tensor_copy(one_r[:, :], ones_row[:, :]).then_inc(tgbo_ready, 1)
                for g in groups[EARLY:]:
                    group(*g)

            def step(s, par):
                t = s - LAG
                if active(t):
                    tile = xt[:, ds(t, 1), :].rearrange("p o d -> p (o d)")
                    dve.wait_ge(out_done, t + 1)
                    nc.vector.tensor_tensor(tile, ps[:, 6, D:2 * D], tile, ALU.add).then_inc(x1a_done, 1)
                    dve.wait_ge(x1a_done, t + 1)
                    nc.vector.tensor_tensor(tile, ps[:, 6, 0:D], tile, ALU.add).then_inc(x1_done, 1)
                    dve.wait_ge(x1_done, t + 1)
                    nc.vector.bn_stats(stats2[:, ds(t, 1), :].rearrange("p o s -> p (o s)"), tile).then_inc(stats_done, 1)
                t = s - 2
                if active(t):
                    for half in range(2):
                        dve.wait_ge(phi_ready, 2 * t + half + 1)
                        nc.vector.tensor_tensor(pT_lo[:, par, 4 * half:4 * half + 4, :],
                                                ps[:, 4 + half, :].rearrange("p (m i) -> p m i", m=4),
                                                as_f32(pT_hi[:, par, 4 * half:4 * half + 4, :]),
                                                ALU.subtract).then_inc(plo_ready, 1)
                t = s - 1
                if active(t):
                    q = (par - 1) % 2
                    dve.wait_ge(exp_done, t + 1)
                    nc.vector.tensor_reduce(sm[:, q, 0:H // 2], sx[:, q, 0:BANK].rearrange("p (h m) -> p h m", m=M),
                                            AX, ALU.add).then_inc(sum_done, 1)
                    dve.wait_ge(sum_done, t + 1)
                    dve.wait_ge(head_done, t + 1)
                    wait_pos(dve, mul_done, t - 1)
                    nc.vector.reciprocal(rs[:, q, :], sm[:, q, :]).then_inc(recip_done, 1)
                for y in norm_tiles(s):
                    y_low(y, 7, y % 2 * D, norm_tiles(s)[-1] + 1)
                t = s
                if active(t):
                    dve.wait_ge(scores_done, t + 1)
                    sc = ps[:, 2 * par:2 * par + 2, :].rearrange("p a (h m) -> p (a h) m", m=M)
                    nc.vector.tensor_reduce(mx[:, par, :], sc, AX, ALU.max, negate=True).then_inc(max_done, 1)
                t = s + 1
                if active(t):
                    q = (par + 1) % 2
                    dve.wait_ge(xhi_ready, t + 1)
                    nc.vector.tensor_tensor(xT_lo[:, q, :, :], ps[:, 7, 0:D].rearrange("p (k i) -> p k i", k=KD),
                                            as_f32(xT_hi[:, q, :, :]), ALU.subtract).then_inc(xlo_ready, 1)
                t = s
                if active(t):
                    dve.wait_ge(max_done, t + 1)
                    wait_pos(dve, pT_done, 2 * (t - 1))
                    nc.vector.tensor_tensor(sx[:, par, 0:BANK].rearrange("p (h m) -> p h m", m=M),
                                            sc[:, 0:H // 2, :],
                                            mx[:, par, 0:H // 2].unsqueeze(2).broadcast_to([P, H // 2, M]),
                                            ALU.add).then_inc(sub_done, 1)
                if isinstance(s, int):
                    if 1 <= s <= 3:
                        x_norm(1, [(0,), (1, 2), (3,)][s - 1])
                    for y in norm_tiles(s + 1):
                        y_tile(y, 2 * (s + 1 - Y_FROM))
            def y_tile(t, done):
                wait_pos(dve, yT_done, done)
                nc.vector.tensor_scalar(yb[:, t % 2, :], xt[:, t, :], mean2[:, t:t + 1], rstd2[:, t:t + 1],
                                        ALU.subtract, ALU.mult).then_inc(y_ready, 1)

            def y_low(t, bank, c0, until):
                dve.wait_ge(yhi_ready, until)
                nc.vector.tensor_tensor(yT_lo[:, :, t * P:(t + 1) * P],
                                        ps[:, bank, c0:c0 + D].rearrange("p (k i) -> p k i", k=KD),
                                        as_f32(yT_hi[:, :, t * P:(t + 1) * P]), ALU.subtract).then_inc(ylo_ready, 1)

            def norm_begins():
                dve.wait_ge(stats_done, NT + TB)
                norm(0, mean2, rstd2)
                for y in norm_tiles(Y_FROM):
                    y_tile(y, 0)

            def route_means(b):
                link(nc.vector.tensor_reduce(rep[:, :, b:b + 1], ysum[:, :, b * TB:(b + 1) * TB], AX, ALU.add))
                nc.vector.tensor_scalar(rep[:, :, b:b + 1], rep[:, :, b:b + 1], 1.0 / S, None,
                                        ALU.mult).then_inc(rep_ready, 1)

            def route_max(b):
                dve.wait_ge(logits_done, b + 1)
                lg = ps[0:1, LOGITS[b], 0:E]
                link(nc.vector.tensor_reduce(row[:, 10, 0:1], lg, AX, ALU.max))
                nc.vector.tensor_scalar(row[:, 1, :], lg, row[:, 10, 0:1], None, ALU.subtract).then_inc(route_sub, 1)

            def route_probs(b):
                dve.wait_ge(route_exp, b + 1)
                link(nc.vector.tensor_reduce(row[:, 11, 0:1], row[:, 2, :], AX, ALU.add))
                link(nc.vector.reciprocal(row[:, 12, 0:1], row[:, 11, 0:1]))
                link(nc.vector.tensor_scalar(row[:, 3, :], row[:, 2, :], row[:, 12, 0:1], None, ALU.mult))
                link(nc.vector.max(row[:, 4, :], row[:, 3, :]))
                nc.vector.max_index(idx[:, b, :], row[:, 4, :], row[:, 3, :]).then_inc(idx_ready, 1)

            def route_shares(b):
                link(nc.vector.tensor_tensor(row[:, 7, 0:1], row[:, 4, 0:1], row[:, 4, 1:2], ALU.add))
                dve.wait_ge(idx_ready, b + 1)
                nc.vector.tensor_copy(row[:, 6, :], idx[:, b, :])
                link(nc.vector.reciprocal(row[:, 8, 0:1], row[:, 7, 0:1]))
                link(nc.vector.tensor_scalar(row[:, 9, 0:TOP], row[:, 4, 0:TOP], row[:, 8, 0:1], None, ALU.mult))
                link(nc.vector.tensor_scalar(row[:, 13, 0:TOP], row[:, 9, 0:TOP], tg[0:1, 1:2], None, ALU.mult))
                for slot in range(TOP):
                    last = nc.vector.tensor_scalar(hot[:, slot, :], iota_row[:, :], row[:, 6, slot:slot + 1],
                                                   None, ALU.is_equal)
                link(last)
                link(nc.vector.tensor_scalar(hot[:, TOP, :], hot[:, 0, :], row[:, 13, 0:1], None, ALU.mult))
                nc.vector.scalar_tensor_tensor(hot[:, TOP, :], hot[:, 1, :], row[:, 13, 1:2], hot[:, TOP, :],
                                               ALU.mult, ALU.add).then_inc(hot_ready, 1)

            def route_read(b):
                dve.wait_ge(hotT_done, b + 1)
                nc.vector.tensor_copy(hotT[:, :], ps[0:E, LOGITS[b], 16:16 + TOP + 1]).then_inc(hotT_ready, 1)

            def route_picked(b):
                dve.wait_ge(sel_done, b + 1)
                sel = ps[:, LOGITS[b] + 1, :]
                nc.vector.tensor_copy(b1sel[:, b, :, :], sel[:, 0:NF * TOP].rearrange("p (f q) -> p f q", q=TOP))
                nc.vector.tensor_copy(b2sel[:, b, :], sel[:, 32:32 + KD])
                link(nc.vector.tensor_copy(swt[:, b * TOP:(b + 1) * TOP], sel[:, 64:64 + TOP]))
                dve.sem_inc(sel_ready, 1)

            def route_first():
                route_means(0)
                route_max(0)

            def w2_low(half):
                rows = slice(half * NF // 2, (half + 1) * NF // 2)
                dve.wait_ge(w_hi_done, 2 + half + 1)
                nc.vector.scalar_tensor_tensor(w2_lo[0][:, rows, :], stage_w2[0][:, rows, :], swt[:, 0:1],
                                               as_f32(w2_hi[0][:, rows, :]), ALU.mult,
                                               ALU.subtract).then_inc(w_lo_done, 1)

            def before_last(s):
                if s == ROUTE_AT + 1:
                    route_probs(0)
                    route_shares(0)
                    route_read(0)
                if s == NT + LAG - 1:
                    route_picked(0)
                    for half in range(2):
                        cols = slice(half * F // 2, (half + 1) * F // 2)
                        dve.wait_ge(w_hi_done, half + 1)
                        nc.vector.tensor_tensor(w1_lo[0][:, :, cols], stage_w1[0][:, :, cols],
                                                as_f32(w1_hi[0][:, :, cols]), ALU.subtract).then_inc(w_lo_done, 1)
                    w2_low(0)

            run_steps(dve, step, value_groups, norm_begins, route_first, before_last)

            def along_expert_0(n):
                if n == 0:
                    w2_low(1)
                    dve.wait_ge(stats_done, 2 * NT)
                if 1 <= n <= 3:
                    norm(1, mean2, rstd2, [(0,), (1,), (2, 3)][n - 1])
                if n == 3:
                    dve.sem_inc(ln_ready, 1)
                for t in y1_tiles(n):
                    y_low(t, 6 + t % 2, 0, t + 1)
                if n == MEANS_AT:
                    route_means(1)
                if n == LOGITS_AT:
                    route_max(1)
                if n == PROBS_AT:
                    route_probs(1)
                if n == SHARES_AT:
                    route_shares(1)
                if n == SELECT_AT:
                    route_read(1)

            def second_residual(pair):
                tiles = xt[:, 2 * pair:2 * pair + 2, :]
                dve.wait_ge(oTT_done, pair + 1)
                nc.vector.tensor_tensor(tiles, ps[:, 6 + pair % 2, :].rearrange("p (t d) -> p t d", t=2), tiles,
                                        ALU.add).then_inc(x2_done, 1)

            def finish(b, c):
                sum_is_through(dve, b, c)
                nc.vector.tensor_scalar(oT[:, 1, c * CH:(c + 1) * CH], ps[:, 2 * c + 1, :], b2sel[:, b, 1:2],
                                        None, ALU.add).then_inc(oT1_ready, 1)

            dve.sem_inc(hlo_ready, FREE_GELS)
            for q in range(NQ):
                b, slot = q // TOP, q % TOP
                if slot == 0 and b > 0:
                    for c in range(NCH):
                        finish(b - 1, c)
                def chunk(c):
                    for f in range(NF):
                        n = (c + q * NCH) * NF + f
                        dve.wait_ge(gelu_done, n + 1 + FREE_BANKS)
                        dve.wait_ge(w2_done, n + 1)
                        nc.vector.tensor_copy(h_hi[:, f % 4, :], gel[:, f % 2, :]).then_inc(hhi_ready, 1)
                        dve.wait_ge(hhi_ready, n + 1)
                        nc.vector.tensor_tensor(h_lo[:, f % 4, :], gel[:, f % 2, :], as_f32(h_hi[:, f % 4, :]),
                                                ALU.subtract).then_inc(hlo_ready, 1)
                        for pc, pf in pieces(q, c, f):
                            nxt, i = 1 - slot, (pc + q * NCH) * NF + pf
                            dve.wait_ge(w_hi_done, PIECES0 + i * 2 + 1)
                            nc.vector.tensor_tensor(w1_lo[nxt][:, ds(pc, 1), pf * P:(pf + 1) * P],
                                                    stage_w1[nxt][:, ds(pc, 1), pf * P:(pf + 1) * P],
                                                    as_f32(w1_hi[nxt][:, ds(pc, 1), pf * P:(pf + 1) * P]),
                                                    ALU.subtract).then_inc(w_lo_done, 1)
                            dve.wait_ge(w_hi_done, PIECES0 + i * 2 + 2)
                            nc.vector.scalar_tensor_tensor(w2_lo[nxt][:, pf, ds(pc * P, P)],
                                                           stage_w2[nxt][:, pf, ds(pc * P, P)], swt[:, q + 1:q + 2],
                                                           as_f32(w2_hi[nxt][:, pf, ds(pc * P, P)]), ALU.mult,
                                                           ALU.subtract).then_inc(w_lo_done, 1)
                        if q == 0:
                            along_expert_0(n)
                        if q == NQ - 1:
                            if (c, f) == FINISH_AT:
                                finish(B - 1, 0)
                            if back_pair(c, f) is not None:
                                second_residual(back_pair(c, f))
                over_chunks(dve, q, chunk)
                if q == 0:
                    route_picked(1)
            finish(B - 1, 1)
            for pair in range(NT // 2 - 2, NT // 2):
                second_residual(pair)

        @block.tensor
        def _(pe):
            mm = nc.tensor.matmul
            pe.wait_ge(ident_ready, 1)

            def three(acc, hi_w, lo_w, hi_x, lo_x, start, stop):
                mm(acc, hi_w, hi_x, start=start, stop=False)
                mm(acc, hi_w, lo_x, start=False, stop=False)
                return mm(acc, lo_w, hi_x, start=False, stop=stop)

            def group(kind, i):
                n = number[(kind, i)]
                bank = ps[:, GRP_BANK[(kind, i)], :]
                if GRP_BEFORE[(kind, i)]:
                    wait_group_read(pe, *GRP_BEFORE[(kind, i)])
                if kind == "ctxT":
                    pe.wait_ge(ld_ctx, 16)
                    for k in range(KD):
                        last = nc.tensor.transpose(bank[:, k * P:(k + 1) * P], ctx_sb[:, k * P:(k + 1) * P], ident[:, :])
                if kind in ("kT", "vT"):
                    w_sb = wk_sb if kind == "kT" else wv_sb
                    pe.wait_ge(ld_wk if kind == "kT" else ld_wv, 16)
                    wait_group_read(pe, "ctxT", 0)
                    for m in range(4):
                        for k in range(KD):
                            c0 = (4 * i + m) * P
                            last = mm(bank[:, m * P:(m + 1) * P], w_sb[:, k, c0:c0 + P], ctxT[:, k, :],
                                      start=(k == 0), stop=(k == KD - 1))
                if kind == "wqT":
                    pe.wait_ge(ld_wq, 16)
                    for m in range(2):
                        for k in range(KD):
                            c0 = (2 * i + m) * P
                            last = nc.tensor.transpose(bank[:, (m * KD + k) * P:(m * KD + k + 1) * P],
                                                       wq_sb[:, k, c0:c0 + P], ident[:, :])
                if kind == "A":
                    ct, mp = i // 4, i % 4
                    wait_group_read(pe, "kT", mp // 2)
                    wait_group_read(pe, "wqT", mp)
                    for m in range(2):
                        last = mm(bank[:, m * B * P:(m + 1) * B * P], wqT[:, 2 * mp + m, ct * P:(ct + 1) * P],
                                  kbd[:, 2 * mp + m, :, :].rearrange("p b x -> p (b x)"), start=True, stop=True)
                if kind == "VW":
                    b, mp = i // 4, i % 4
                    pe.wait_ge(ld_wo, 16)
                    wait_group_read(pe, "vT", mp // 2)
                    for m in range(2):
                        last = mm(bank[:, m * D:(m + 1) * D], vbd[:, 2 * mp + m, b, :], wo_sb[:, 2 * mp + m, :],
                                  start=True, stop=True)
                last.then_inc(grp_done, 1)
            for g in groups[:EARLY]:
                group(*g)
            wait_group_read(pe, "A", 0)

            def value_groups():
                for g in groups[EARLY:]:
                    group(*g)

            def step(s, par):
                t = s - 2
                if active(t):
                    pe.wait_ge(mul_done, t + 1)
                    for half in range(2):
                        wait_pos(pe, plo_ready, 2 * t + half - 1)
                        for m in range(4):
                            c0 = (4 * half + m) * P
                            last = nc.tensor.transpose(ps[:, 4 + half, m * P:(m + 1) * P],
                                                       sx[:, par, c0:c0 + P], ident[:, :])
                        last.then_inc(pT_done, 1)
                if isinstance(s, int) and s == ROUTE_AT + 1:
                    route_pick(0)
                for y in norm_tiles(s):
                    pe.wait_ge(xlo_ready, min(s + 1, NT))
                    y_transpose(y, 7, y % 2 * D)
                if isinstance(s, int) and s == 0:
                    wait_group_read(pe, "A", 7)
                t = s
                if active(t):
                    pe.wait_ge(xlo_ready, t + 1)
                    wait_pos(pe, sub_done, t - 1)
                    wait_pos(pe, head_done, t - 1)
                    boff = (t // TB) * HM
                    for c in range(2):
                        for k in range(KD):
                            lo, hi = xT_lo[:, par, k, :], xT_hi[:, par, k, :]
                            wh, wl = (w[:, k, ds(boff + c * BANK, BANK)] for w in (a_hi, a_lo))
                            last = three(ps[:, 2 * par + c, :], hi, lo, wh, wl, k == 0, k == KD - 1)
                    last.then_inc(scores_done, 1)
                t = s + 1
                if active(t):
                    q = (par + 1) % 2
                    pe.wait_ge(xn_ready, t + 1)
                    wait_pos(pe, xlo_ready, t)
                    if len(norm_tiles(s)):
                        pe.wait_ge(ylo_ready, norm_tiles(s)[-1] + 1)
                    for k in range(KD):
                        last = nc.tensor.transpose(ps[:, 7, k * P:(k + 1) * P], xn[:, q, k * P:(k + 1) * P], ident[:, :])
                    last.then_inc(xT_done, 1)
                t = s - 2
                if active(t):
                    wait_pos(pe, x1_done, t)
                    bm = (t // TB) * NP
                    if isinstance(t, int) and t == 0:
                        pe.wait_ge(tgbo_ready, 3)
                    mm(ps[:, 6, :], one_r[:, :], bo_parts[:, :], start=True, stop=False)
                    for m in range(NP):
                        if m % 4 == 0:
                            pe.wait_ge(plo_ready, 2 * t + m // 4 + 1)
                        mm(ps[:, 6, :], pT_hi[:, par, m, :], vw[:, ds(bm + m, 1), :].rearrange("p o n -> p (o n)"),
                           start=False, stop=False)
                        last = mm(ps[:, 6, 0:D], pT_lo[:, par, m, :],
                                  vw[:, ds(bm + m, 1), 0:D].rearrange("p o n -> p (o n)"),
                                  start=False, stop=(m == NP - 1))
                    last.then_inc(out_done, 1)
            def y_transpose(t, bank, c0):
                pe.wait_ge(y_ready, t + 1)
                for k in range(KD):
                    last = nc.tensor.transpose(ps[:, bank, c0 + k * P:c0 + (k + 1) * P],
                                               yb[:, t % 2, k * P:(k + 1) * P], ident[:, :])
                last.then_inc(yT_done, 1)

            def route(b):
                pe.wait_ge(rep_ready, b + 1)
                for k in range(KD):
                    last = mm(ps[0:1, LOGITS[b], 0:E], rep[:, k, b:b + 1], gate_sb[:, k, :],
                              start=(k == 0), stop=(k == KD - 1))
                last.then_inc(logits_done, 1)

            def route_select(b):
                pe.wait_ge(hot_ready, b + 1)
                for r in range(TOP + 1):
                    last = mm(ps[0:E, LOGITS[b], 16 + r:17 + r], hot[:, r, :], ones_row[0:1, 0:1],
                              start=True, stop=True)
                last.then_inc(hotT_done, 1)

            def route_pick(b):
                pe.wait_ge(hotT_ready, b + 1)
                pe.wait_ge(ld_b12, 32)
                sel = ps[:, LOGITS[b] + 1, :]
                for f in range(NF):
                    mm(sel[:, f * TOP:(f + 1) * TOP], b1_sb[:, f * P:(f + 1) * P], hotT[:, 0:TOP], start=True, stop=True)
                for k in range(KD):
                    mm(sel[:, 32 + k:33 + k], b2_sb[:, k * P:(k + 1) * P], hotT[:, TOP:TOP + 1], start=True, stop=True)
                mm(sel[:, 64:64 + TOP], ones_row[:, :], row[:, 13, 0:TOP], start=True, stop=True).then_inc(sel_done, 1)

            def route_first():
                pe.wait_ge(sub_done, NT - 1)
                pe.wait_ge(head_done, NT - 1)
                pe.wait_ge(ylo_ready, TB)
                route(0)

            def before_last(s):
                if s == ROUTE_AT + 1:
                    route_select(0)

            run_steps(pe, step, value_groups, route=route_first, before_last=before_last)

            pe.wait_ge(sub_done, NT)
            pe.wait_ge(head_done, NT)
            pe.wait_ge(plo_ready, 2 * NT)
            pe.wait_ge(sel_ready, 1)
            pe.sem_inc(w2_done, FREE_SPLITS)

            def first_layer(q, c, f):
                slot, n = q % TOP, (c + q * NCH) * NF + f
                tok = (c + q // TOP * NCH) * CH
                pe.wait_ge(gelu_done, n + 1)
                for k in range(KD):
                    hi, lo = (w[slot][:, k, f * P:(f + 1) * P] for w in (w1_hi, w1_lo))
                    last = three(ps[:, 4 + f % 2, :], hi, lo, yT_hi[:, k, ds(tok, CH)], yT_lo[:, k, ds(tok, CH)],
                                 k == 0, k == KD - 1)
                last.then_inc(h_done, 1)

            def second_layer(q, c, f):
                slot, n = q % TOP, (c + q * NCH) * NF + f
                if f == 0 and q >= TOP:
                    pe.wait_ge(oT0_ready, q // TOP * NCH)
                    pe.wait_ge(oT1_ready, q // TOP * NCH)
                pe.wait_ge(hlo_ready, n + 1 + FREE_GELS)
                for d in range(KD):
                    hi, lo = (w[slot][:, f, d * P:(d + 1) * P] for w in (w2_hi, w2_lo))
                    acc = ps[:, ds(c * KD + d, 1), :].rearrange("p o n -> p (o n)")
                    last = three(acc, hi, lo, h_hi[:, f % 4, :], h_lo[:, f % 4, :],
                                 slot == 0 and f == 0, slot == TOP - 1 and f == NF - 1)
                last.then_inc(w2_done, 1)

            def back(pair):
                c = pair // (CH // P // 2)
                pe.wait_ge(oT0_ready, c + 1)
                pe.wait_ge(oT1_ready, c + 1)
                if pair >= 2:
                    pe.wait_ge(x2_done, pair - 1)
                for j in range(2 * KD):
                    t0 = (2 * pair + j // KD) * P % S
                    last = nc.tensor.transpose(ps[:, 6 + pair % 2, j * P:(j + 1) * P],
                                               oT[:, j % KD, t0:t0 + P], ident[:, :])
                last.then_inc(oTT_done, 1)

            def along_expert_0(n):
                for t in y1_tiles(n):
                    if t == TB:
                        pe.wait_ge(x1_done, NT)
                        pe.wait_ge(xlo_ready, NT)
                        pe.wait_ge(ylo_ready, TB)
                    if t >= TB + 2:
                        pe.wait_ge(ylo_ready, t - 1)
                    y_transpose(t, 6 + t % 2, 0)
                if n == LOGITS_AT:
                    pe.wait_ge(ylo_ready, NT)
                    route(1)
                if n == SELECT_AT:
                    route_select(1)

            for q in range(NQ):
                b, slot = q // TOP, q % TOP
                def chunk(c):
                    if q > 0:
                        pe.wait_ge(w_lo_done, q * (2 * NCH * NF) + PIECES0)
                    for f in range(NF):
                        if q == 0 and c == 0 and f % (NF // 2) == 0:
                            pe.wait_ge(w_lo_done, f // (NF // 2) + 1)
                        first_layer(q, c, f)
                        if q == 0:
                            along_expert_0(c * NF + f)
                        if q == NQ - 1 and back_pair(c, f) is not None:
                            back(back_pair(c, f))
                        if q == 0 and c == 0 and f in (2, NF // 2 + 2):
                            pe.wait_ge(w_lo_done, 3 if f == 2 else PIECES0)
                        if f >= 2:
                            second_layer(q, c, f - 2)
                    second_layer(q, c, NF - 2)
                    second_layer(q, c, NF - 1)
                over_chunks(pe, q, chunk)
                if q == 0:
                    route_pick(1)
            for pair in range(NT // 2 - 2, NT // 2):
                back(pair)

_INS = ["x", "ctx_1024", "g_xattn", "g_ffn", "L0_xattn_Wq", "L0_xattn_Wk", "L0_xattn_Wv", "L0_xattn_Wo",
        "L0_xattn_bo", "L0_ffn_gate_w", "L0_ffn_w1", "L0_ffn_b1", "L0_ffn_w2", "L0_ffn_b2"]


def kernel(**inputs):
    import numpy as _np
    import concourse.bacc as _bacc
    from concourse import mybir as _mybir
    from concourse.bass_utils import run_bass_kernel_spmd as _run

    nc = _bacc.Bacc("TRN2", target_bir_lowering=False, num_devices=1)
    arrays, args = {}, []
    for name in _INS:
        a = _np.ascontiguousarray(inputs[name])
        arrays[f"in_{name}_dram"] = a
        args.append(nc.dram_tensor(f"in_{name}_dram", a.shape, _mybir.dt.from_np(a.dtype), kind="ExternalInput").ap())
    shape = inputs["x"].shape
    out = nc.dram_tensor("out_0_dram", (shape[0] * shape[1], shape[2]), _mybir.dt.float32,
                         kind="ExternalOutput").ap()
    gated_cross_attention_moe_kernel(nc, *args, out)
    r = _run(nc, [arrays], core_ids=[0])
    return r.results[0]["out_0_dram"].reshape(shape)
```
